# Optimizing a Trainium2 kernel written in Bass

```python
import numpy as np
import jax
import jax.numpy as jnp

def _softmax(x, axis=-1):
    return jax.nn.softmax(x, axis=axis)

def _gelu(x):
    return jax.nn.gelu(x, approximate=True)

def _silu(x):
    return jax.nn.silu(x)

def _sigmoid(x):
    return jax.nn.sigmoid(x)

def _layernorm(x, axis=-1, eps=1e-05):
    m = jnp.mean(x, axis=axis, keepdims=True)
    v = jnp.var(x, axis=axis, keepdims=True)
    return (x - m) / jnp.sqrt(v + eps)

def _scatter_add(tgt, idx, src, axis=0):
    return tgt.at[idx].add(src)

def _segment_sum(src, seg, n):
    return jax.ops.segment_sum(src, seg, n)
kernel_name = 'mk_seq_preln_d1_jaxref_r8_1b211a'

def setup_inputs(seed: int=0):
    np.random.seed(seed)
    _w = jnp.asarray

    def _L0_attn_setup():
        import jax, jax.numpy as jnp
        import numpy as np
        from jax.scipy.linalg import solve_triangular
        B, T, D = (2, 512, 128)
        HEAD_DIM = 128
        CHUNK = 64

        def _forward(out, W_write, W_read, W_alpha, W_beta, A_log, dt_bias):
            Bs, Ts, Ds = out.shape
            d, C = (HEAD_DIM, CHUNK)
            H = Ds // d
            x = out.astype(jnp.float32)
            rk = x.reshape(Bs, Ts, H, d)
            rk = rk / jnp.maximum(jnp.linalg.norm(rk, axis=-1, keepdims=True), 1e-12)
            rk = jnp.swapaxes(rk, 1, 2)
            wk = jnp.pad(rk[:, :, :-1], ((0, 0), (0, 0), (1, 0), (0, 0)))
            v = jnp.einsum('btd,ed->bte', x, W_write).reshape(Bs, Ts, H, d)
            v = jnp.swapaxes(v, 1, 2)
            beta = jax.nn.sigmoid(jnp.einsum('btd,hd->bth', x, W_beta))
            beta = jnp.swapaxes(beta, 1, 2)[..., None]
            log_decay = -jnp.exp(A_log)[None, None, :] * jax.nn.softplus(jnp.einsum('btd,hd->bth', x, W_alpha) + dt_bias)
            log_decay = jnp.swapaxes(log_decay, 1, 2)
            v_scaled = v * beta
            wk_scaled = wk * beta
            pad = -Ts % C
            if pad:
                p4 = ((0, 0), (0, 0), (0, pad), (0, 0))
                rk = jnp.pad(rk, p4)
                wk = jnp.pad(wk, p4)
                v_scaled = jnp.pad(v_scaled, p4)
                wk_scaled = jnp.pad(wk_scaled, p4)
                log_decay = jnp.pad(log_decay, ((0, 0), (0, 0), (0, pad)))
            Tp = Ts + pad
            N = Tp // C
            chunk = lambda a: a.reshape(Bs, H, N, C, d)
            rk, wk, v_scaled, wk_scaled = map(chunk, (rk, wk, v_scaled, wk_scaled))
            log_decay = log_decay.reshape(Bs, H, N, C)
            cum = jnp.cumsum(log_decay, -1)
            L_mask = jnp.tril(jnp.exp(jnp.tril(cum[..., :, None] - cum[..., None, :])))
            decay_exp = jnp.exp(cum)[..., None]
            chunk_end_decay = jnp.exp(cum[..., -1])
            M = jnp.tril(-(wk_scaled @ jnp.swapaxes(wk, -1, -2)) * L_mask, -1)
            eye = jnp.eye(C, dtype=x.dtype)
            A = solve_triangular(eye - M, jnp.broadcast_to(eye, M.shape), lower=True, unit_diagonal=True)
            intra = jnp.tril(rk @ jnp.swapaxes(wk, -1, -2) * L_mask, -1)
            rk_decay = rk * decay_exp
            tail_decay = jnp.exp(cum[..., -1:] - cum)[..., None]
            wk_pos = jnp.swapaxes(wk * tail_decay, -1, -2)
            wk_scaled_dec = wk_scaled * decay_exp
            toN = lambda a: jnp.moveaxis(a, 2, 0)

            def step(S, inp):
                A_i, vsc_i, wkd_i, rkd_i, intra_i, wkp_i, ced_i = inp
                v_new = A_i @ vsc_i - A_i @ wkd_i @ S
                o_i = rkd_i @ S + intra_i @ v_new
                S = ced_i[..., None, None] * S + wkp_i @ v_new
                return (S, o_i)
            S0 = jnp.zeros((Bs, H, d, d), x.dtype)
            _, o = jax.lax.scan(step, S0, (toN(A), toN(v_scaled), toN(wk_scaled_dec), toN(rk_decay), toN(intra), toN(wk_pos), jnp.moveaxis(chunk_end_decay, 2, 0)))
            o = jnp.moveaxis(o, 0, 2).reshape(Bs, H, Tp, d)
            o = jnp.swapaxes(o, 1, 2).reshape(Bs, Tp, Ds)[:, :Ts]
            return out + jnp.einsum('btd,ed->bte', o, W_read).astype(out.dtype)
        key = jax.random.key(seed)
        ks = jax.random.split(key, 7)
        H = D // HEAD_DIM
        out = jax.random.normal(ks[0], (B, T, D), dtype=jnp.float32)
        scale = D ** (-0.5)
        W_write = jax.random.normal(ks[1], (D, D), jnp.float32) * scale
        W_read = jax.random.normal(ks[2], (D, D), jnp.float32) * scale
        W_alpha = jax.random.normal(ks[3], (H, D), jnp.float32) * scale
        W_beta = jax.random.normal(ks[4], (H, D), jnp.float32) * scale
        A_log = jnp.log(jax.random.uniform(ks[5], (H,), jnp.float32, 0.05, 16.0))
        dt_bias = jnp.ones((H,), jnp.float32)
        return {'out': out, 'W_write': W_write, 'W_read': W_read, 'W_alpha': W_alpha, 'W_beta': W_beta, 'A_log': A_log, 'dt_bias': dt_bias}
    _L0_attn_in = _L0_attn_setup()

    def _L0_ffn_setup():
        import jax, jax.numpy as jnp
        import numpy as np
        TOP_P = 0.8
        B, T, H, F, E = (2, 256, 128, 512, 8)
        key = jax.random.key(seed)
        k0, k1, k2, k3 = jax.random.split(key, 4)
        x = jax.random.normal(k0, (B, T, H), jnp.float32)
        Wr = jax.random.normal(k1, (H, E), jnp.float32) * 0.02
        br = jnp.zeros((E,), jnp.float32)
        W1 = jax.random.normal(k2, (E, H, F), jnp.float32) * 0.02
        b1 = jnp.zeros((E, F), jnp.float32)
        W2 = jax.random.normal(k3, (E, F, H), jnp.float32) * 0.02
        b2 = jnp.zeros((E, H), jnp.float32)
        return {'x': x, 'Wr': Wr, 'br': br, 'W1': W1, 'b1': b1, 'W2': W2, 'b2': b2}
    _L0_ffn_in = _L0_ffn_setup()
    _d = {'L0_attn_out': _L0_attn_in['out'], 'L0_attn_W_write': _L0_attn_in['W_write'], 'L0_attn_W_read': _L0_attn_in['W_read'], 'L0_attn_W_alpha': _L0_attn_in['W_alpha'], 'L0_attn_W_beta': _L0_attn_in['W_beta'], 'L0_attn_A_log': _L0_attn_in['A_log'], 'L0_attn_dt_bias': _L0_attn_in['dt_bias'], 'L0_ffn_Wr': _L0_ffn_in['Wr'], 'L0_ffn_br': _L0_ffn_in['br'], 'L0_ffn_W1': _L0_ffn_in['W1'], 'L0_ffn_b1': _L0_ffn_in['b1'], 'L0_ffn_W2': _L0_ffn_in['W2'], 'L0_ffn_b2': _L0_ffn_in['b2']}
    _x0 = _d['L0_attn_out']
    _d['L0_attn_out'] = jax.random.normal(jax.random.fold_in(jax.random.key(seed), 1), (8, 512, 128), dtype=_x0.dtype)
    del _x0
    return _d

def reference(L0_attn_out, L0_attn_W_write, L0_attn_W_read, L0_attn_W_alpha, L0_attn_W_beta, L0_attn_A_log, L0_attn_dt_bias, L0_ffn_Wr, L0_ffn_br, L0_ffn_W1, L0_ffn_b1, L0_ffn_W2, L0_ffn_b2):

    def _L0_attn_ref(out, W_write, W_read, W_alpha, W_beta, A_log, dt_bias):
        import jax, jax.numpy as jnp
        import numpy as np
        from jax.scipy.linalg import solve_triangular
        B, T, D = (2, 512, 128)
        HEAD_DIM = 128
        CHUNK = 64

        def _forward(out, W_write, W_read, W_alpha, W_beta, A_log, dt_bias):
            Bs, Ts, Ds = out.shape
            d, C = (HEAD_DIM, CHUNK)
            H = Ds // d
            x = out.astype(jnp.float32)
            rk = x.reshape(Bs, Ts, H, d)
            rk = rk / jnp.maximum(jnp.linalg.norm(rk, axis=-1, keepdims=True), 1e-12)
            rk = jnp.swapaxes(rk, 1, 2)
            wk = jnp.pad(rk[:, :, :-1], ((0, 0), (0, 0), (1, 0), (0, 0)))
            v = jnp.einsum('btd,ed->bte', x, W_write).reshape(Bs, Ts, H, d)
            v = jnp.swapaxes(v, 1, 2)
            beta = jax.nn.sigmoid(jnp.einsum('btd,hd->bth', x, W_beta))
            beta = jnp.swapaxes(beta, 1, 2)[..., None]
            log_decay = -jnp.exp(A_log)[None, None, :] * jax.nn.softplus(jnp.einsum('btd,hd->bth', x, W_alpha) + dt_bias)
            log_decay = jnp.swapaxes(log_decay, 1, 2)
            v_scaled = v * beta
            wk_scaled = wk * beta
            pad = -Ts % C
            if pad:
                p4 = ((0, 0), (0, 0), (0, pad), (0, 0))
                rk = jnp.pad(rk, p4)
                wk = jnp.pad(wk, p4)
                v_scaled = jnp.pad(v_scaled, p4)
                wk_scaled = jnp.pad(wk_scaled, p4)
                log_decay = jnp.pad(log_decay, ((0, 0), (0, 0), (0, pad)))
            Tp = Ts + pad
            N = Tp // C
            chunk = lambda a: a.reshape(Bs, H, N, C, d)
            rk, wk, v_scaled, wk_scaled = map(chunk, (rk, wk, v_scaled, wk_scaled))
            log_decay = log_decay.reshape(Bs, H, N, C)
            cum = jnp.cumsum(log_decay, -1)
            L_mask = jnp.tril(jnp.exp(jnp.tril(cum[..., :, None] - cum[..., None, :])))
            decay_exp = jnp.exp(cum)[..., None]
            chunk_end_decay = jnp.exp(cum[..., -1])
            M = jnp.tril(-(wk_scaled @ jnp.swapaxes(wk, -1, -2)) * L_mask, -1)
            eye = jnp.eye(C, dtype=x.dtype)
            A = solve_triangular(eye - M, jnp.broadcast_to(eye, M.shape), lower=True, unit_diagonal=True)
            intra = jnp.tril(rk @ jnp.swapaxes(wk, -1, -2) * L_mask, -1)
            rk_decay = rk * decay_exp
            tail_decay = jnp.exp(cum[..., -1:] - cum)[..., None]
            wk_pos = jnp.swapaxes(wk * tail_decay, -1, -2)
            wk_scaled_dec = wk_scaled * decay_exp
            toN = lambda a: jnp.moveaxis(a, 2, 0)

            def step(S, inp):
                A_i, vsc_i, wkd_i, rkd_i, intra_i, wkp_i, ced_i = inp
                v_new = A_i @ vsc_i - A_i @ wkd_i @ S
                o_i = rkd_i @ S + intra_i @ v_new
                S = ced_i[..., None, None] * S + wkp_i @ v_new
                return (S, o_i)
            S0 = jnp.zeros((Bs, H, d, d), x.dtype)
            _, o = jax.lax.scan(step, S0, (toN(A), toN(v_scaled), toN(wk_scaled_dec), toN(rk_decay), toN(intra), toN(wk_pos), jnp.moveaxis(chunk_end_decay, 2, 0)))
            o = jnp.moveaxis(o, 0, 2).reshape(Bs, H, Tp, d)
            o = jnp.swapaxes(o, 1, 2).reshape(Bs, Tp, Ds)[:, :Ts]
            return out + jnp.einsum('btd,ed->bte', o, W_read).astype(out.dtype)
        return _forward(out, W_write, W_read, W_alpha, W_beta, A_log, dt_bias)

    def _L0_ffn_ref(x, Wr, br, W1, b1, W2, b2):
        import jax, jax.numpy as jnp
        import numpy as np
        TOP_P = 0.8
        B, T, H, F, E = (2, 256, 128, 512, 8)
        probs = jax.nn.softmax(x @ Wr + br, axis=-1)
        sorted_idx = jnp.argsort(-probs, axis=-1)
        sorted_probs = jnp.take_along_axis(probs, sorted_idx, axis=-1)
        cum = jnp.cumsum(sorted_probs, axis=-1)
        mask = cum < TOP_P
        mask = mask.at[..., 0].set(True)
        inv = jnp.argsort(sorted_idx, axis=-1)
        keep = jnp.take_along_axis(mask, inv, axis=-1)
        gate = probs * keep
        h = jax.nn.relu(jnp.einsum('bth,ehf->betf', x, W1) + b1[None, :, None, :])
        y = jnp.einsum('betf,efh->beth', h, W2) + b2[None, :, None, :]
        return jnp.einsum('bte,beth->bth', gate, y)
    x = L0_attn_out
    x = x + _L0_attn_ref(_layernorm(x, axis=-1), L0_attn_W_write, L0_attn_W_read, L0_attn_W_alpha, L0_attn_W_beta, L0_attn_A_log, L0_attn_dt_bias)
    x = x + _L0_ffn_ref(_layernorm(x, axis=-1), L0_ffn_Wr, L0_ffn_br, L0_ffn_W1, L0_ffn_b1, L0_ffn_W2, L0_ffn_b2)
    return x

_drawn_inputs = setup_inputs


def setup_inputs(seed=0):
    import zlib

    import numpy as np

    out = dict(_drawn_inputs(seed))
    spreads = {'L0_ffn_br': (0.0, 0.764), 'L0_ffn_b1': (0.0, 0.8), 'L0_ffn_b2': (0.0, 0.533)}
    factors = {'L0_attn_W_write': 8.0,
     'L0_attn_W_read': 8.0,
     'L0_attn_W_alpha': 8.0,
     'L0_attn_W_beta': 8.0,
     'L0_ffn_Wr': 5.046,
     'L0_ffn_W1': 5.599,
     'L0_ffn_W2': 4.427}
    for name, (base, spread) in spreads.items():
        noise = np.random.default_rng([zlib.crc32(name.encode()), seed]).standard_normal(out[name].shape)
        drawn = base * np.exp(spread * noise) if base else spread * noise
        out[name] = jnp.asarray(drawn.astype(out[name].dtype))
    for name, factor in factors.items():
        out[name] = (out[name] * factor).astype(out[name].dtype)
    return out
```

```python
from contextlib import ExitStack

import concourse.bass as bass
from concourse import mybir

P = 128
TILES = 4
LEVELS = 7
LN_EPS = 1e-5
TOP_P = 0.8
X_SCALE = 16.0
FAR = 1e30
RSQRT_SEED = float(0x5F3759DF)

ALU = mybir.AluOpType
ACT = mybir.ActivationFunctionType
AX_X = mybir.AxisListType.X
F32 = mybir.dt.float32
F16 = mybir.dt.float16
BF16 = mybir.dt.bfloat16
I32 = mybir.dt.int32
RMAX = bass.bass_isa.ReduceOp.max


def preln_layer(nc, x_in, W_write, W_read, W_alpha, W_beta, A_log, dt_bias, Wr, br, W1, b1, W2, b2, out):
    B, T, D = x_in.shape
    E, _, F = W1.shape
    N = T // P
    H = B // TILES
    G = N * B
    FB = F // P
    assert D == P and TILES * P == 512 and B == H * TILES and H == 2 and E == 8

    x_v = x_in.rearrange("b (n p) d -> n p b d", p=P)
    out_v = out.rearrange("b (n p) d -> p n b d", p=P)
    row = lambda v: v.rearrange("(a n) -> a n", a=1)

    ctx = ExitStack()
    with ctx:
        def sb(name, shape, dt=F32):
            return ctx.enter_context(nc.sbuf_tensor(name, shape, dt))

        def sem(name):
            return ctx.enter_context(nc.semaphore(name))

        x_all = sb("x_all", [P, N, B, D])
        rkT_all = sb("rkT_all", [P, B, 1 + T])
        w1f = sb("w1f", [P, E, F])
        w2f = sb("w2f", [P, E, FB, D])
        w1p = sb("w1p", [P, 2, E, F], F16)
        w2p = sb("w2p", [P, 2, E, FB, D], F16)
        wrf = sb("wrf", [P, E])
        wrp = sb("wrp", [P, 2, E], F16)
        wwf = sb("wwf", [P, D])
        wof = sb("wof", [P, D])
        WwT = sb("WwT", [P, D])
        WoT = sb("WoT", [P, D])
        wab = sb("wab", [P, 2])
        alog = sb("alog", [P, 1])
        dtb = sb("dtb", [P, 1])
        nega = sb("nega", [P, 1])
        br_bc = sb("br_bc", [P, E])
        b2_sb = sb("b2_sb", [E, D])
        b1r = sb("b1r", [E * FB, P])
        b1s = sb("b1s", [P, E, FB])

        ident = sb("ident", [P, P])
        ident_b = sb("ident_b", [P, P], BF16)
        ones = sb("ones", [P, P])
        upto = sb("upto", [P, P])
        far_b = sb("far_b", [P, P], BF16)
        join = sb("join", [P, LEVELS, P])
        ge_tri = sb("ge_tri", [P, E, E])

        stats = sb("stats", [P, G, 6])
        mv = sb("mv", [P, G, 2])
        sc = {k: sb("sc_" + k, [P, G]) for k in
              ("ve", "rstd", "q", "n2", "rn", "nrm", "f", "one", "mr", "za", "zb", "na", "nb", "ua", "ub",
               "la", "den", "mb", "num", "ld", "cum", "ncum", "tot", "tmc", "dexp", "ndexp", "ced", "tail",
               "beta")}
        z_all = sb("z_all", [P, G, 2])
        wmax = sb("wmax", [P, 8])

        rk = [sb(f"rk{h}", [P, TILES, D]) for h in range(H)]
        rkTs = [sb(f"rkTs{h}", [P, TILES, P]) for h in range(H)]
        wkx = [sb(f"wkx{h}", [P, TILES, P + 1]) for h in range(H)]
        ldU = [sb(f"ldU{h}", [P, TILES, P]) for h in range(H)]
        wkt = [sb(f"wkt{h}", [P, TILES, D]) for h in range(H)]
        expB = [sb(f"expB{h}", [P, TILES, P]) for h in range(H)]
        dec = [sb(f"dec{h}", [P, TILES, P]) for h in range(H)]
        rkd = [sb(f"rkd{h}", [P, TILES, P]) for h in range(H)]
        V = [sb(f"V{h}", [P, TILES, D]) for h in range(H)]
        LT = [sb(f"LT{h}", [P, TILES, P]) for h in range(H)]
        intraT = [sb(f"intraT{h}", [P, TILES, P]) for h in range(H)]
        X = [sb(f"X{h}", [P, TILES, P]) for h in range(H)]
        XT = [sb(f"XT{h}", [P, TILES, P]) for h in range(H)]
        Tn = [sb(f"Tn{h}", [P, TILES, P]) for h in range(H)]
        R = [sb(f"R{h}", [P, TILES, D]) for h in range(H)]
        vnew = [sb(f"vnew{h}", [P, TILES, D]) for h in range(H)]
        oT = [sb(f"oT{h}", [P, TILES, P]) for h in range(H)]
        S = [sb(f"S{h}", [P, TILES, D]) for h in range(H)]

        xn = rk
        xp = [sb(f"xp{h}", [P, 2, TILES, P], F16) for h in range(H)]
        w2words = w2f[:, :, :, :].rearrange("p e c d -> p (e c d)")
        hf = [w2words[:, 512 * i:512 * (i + 1)] for i in range(2)]
        hp = [w1f[:, E // 2 * i:E // 2 * (i + 1), :].rearrange("p e f -> p (e f)").bitcast(F16).rearrange(
            "p (a c t) -> p a c t", a=2, c=FB) for i in range(2)]
        mst = sb("mst", [P, TILES, 6])
        mmv = sb("mmv", [P, TILES, 2])
        mr_ = {k: sb("m_" + k, [P, TILES]) for k in ("ve", "r", "q", "mx", "sum", "rs")}
        lg = sb("lg", [P, TILES, E])
        pe_ = sb("pe_", [P, TILES, E])
        pr = sb("pr", [P, TILES, E])
        cmp1 = sb("cmp1", [P, TILES, E, E])
        cmp2 = sb("cmp2", [P, TILES, E, E])
        cumt = sb("cumt", [P, TILES, E])
        k1 = sb("k1", [P, TILES, E])
        k2 = sb("k2", [P, TILES, E])
        gate = [sb(f"gate{h}", [P, TILES, E]) for h in range(H)]
        gates = [sb(f"gates{h}", [P, TILES, E]) for h in range(H)]
        gT = [sb(f"gT{h}", [E, TILES, P]) for h in range(H)]

        bank = [ctx.enter_context(nc.psum_tensor(f"bank{i}", [P, 512], F32)) for i in range(8)]
        tl = lambda b: bank[b][:, :].rearrange("p (t c) -> p t c", t=TILES)

        def gq(h):
            return [bank[4 * h + 1][:, 0:2 * (P + 1)].rearrange("p (t c) -> p t c", t=2),
                    bank[4 * h + 2][:, 0:2 * (P + 1)].rearrange("p (t c) -> p t c", t=2)]

        x_landed = [sem(f"x_landed{n}") for n in range(N)]
        small_landed = sem("small_landed")
        w1_landed, w2_landed = sem("w1_landed"), sem("w2_landed")
        consts = sem("consts")
        pool_link, dve_link, act_link = sem("pool_link"), sem("dve_link"), sem("act_link")
        zero_done = sem("zero_done")
        wT_ps, wT_sb = sem("wT_ps"), sem("wT_sb")
        b1T_ps = sem("b1T_ps")
        wr_hi = sem("wr_hi")
        stats_done = sem("stats_done")
        rk_made, rkT_ps, rkT_sb, rkT_kept, z_ps, z_sb = (sem(s) for s in ("rk_made", "rkT_ps", "rkT_sb", "rkT_kept", "z_ps", "z_sb"))
        exp_in, exp_out = sem("exp_in"), sem("exp_out")
        ld_ready, cum_ps, cols_ready = sem("ld_ready"), sem("cum_ps"), sem("cols_ready")
        base_ready = sem("base_ready")
        scale_ready = sem("scale_ready")
        att = {k: sem("att_" + k) for k in
               ("wkx", "ldU", "wkT_ps", "wkt", "gq_ps", "B_ps", "expB", "Bm_ps", "dec", "rkd", "V_ps", "V", "WS_ps",
                "R", "LT", "intra", "tmp0", "XT0", "X0_ps", "X0", "T_ps", "Tn", "XC_ps", "XTC_ps", "X", "XT",
                "VN_ps", "vnew", "SN_ps", "S", "OT_ps", "oT", "O_ps", "x1")}
        w_hi, w_lo = sem("w_hi"), sem("w_lo")
        m = {k: sem("moe_" + k) for k in
             ("link", "xn", "xnT_ps", "xhi", "xlo", "lg_ps", "lg", "e", "gate", "gT_ps", "gT", "b2_ps", "acc0",
              "up_ps", "hf", "hhi", "hlo", "dn_ps", "acc", "stored")}

        block = ctx.enter_context(nc.Block())

        def done(n, h, per=1, k=0):
            return n * (H * per) + (h * per + k + 1)

        def lev(n, h, k, levels):
            return n * (H * levels) + (H * k + h + 1)

        col = lambda t, n, h, i: t[:, bass.ds(n * B + (TILES * h + i), 1)]
        cols = lambda t, n, h: t[:, bass.ds(n * B + TILES * h, TILES)]
        bc = lambda a, w: a.unsqueeze(2).to_broadcast([P, TILES, w])
        xg = lambda n, h: x_all[:, bass.ds(n, 1), TILES * h:TILES * h + TILES, :].rearrange("p a b d -> p (a b) d")

        NSMALL = 10

        @block.sync
        def _(sp):
            for n in range(N):
                sp.dma_start(x_all[:, n, :, :], x_v[n]).then_inc(x_landed[n], 16)
            sp.dma_start(w1f[:, :, :], W1.rearrange("e h f -> h e f")).then_inc(w1_landed, 16)
            for e in range(E):
                sp.dma_start(w2f[:, e, :, :], W2[e].rearrange("(c p) h -> p c h", p=P)).then_inc(w2_landed, 16)
            with sp.Fori(0, N) as n:
                for h in range(H):
                    sp.wait_ge(m["acc"], done(n, h, E, E - 1))
                    sp.dma_start(out_v[:, bass.ds(n, 1), TILES * h:TILES * h + TILES, :].rearrange("p a b d -> p (a b) d"),
                                 xg(n, h)).then_inc(m["stored"], 16)
            sp.wait_ge(m["stored"], 16 * N * H)

        @block.gpsimd
        def _(pool):
            count = [0]

            def link(ins):
                count[0] += 1
                ins.then_inc(pool_link, 1)
                pool.wait_ge(pool_link, count[0])

            pool.memset(ones[:, :], 1.0)
            pool.memset(ident[:, :], 0.0)
            pool.memset(ident_b[:, :], 0.0)
            pool.memset(far_b[:, :], 0.0)
            pool.memset(upto[:, :], 1.0)
            pool.memset(ge_tri[:, :, :], 1.0)
            link(pool.memset(join[:, :, :], 0.0))
            for t in (ident, ident_b):
                pool.affine_select(out=t[:, :], in_=t[:, :], compare_op=ALU.not_equal, fill=1.0, base=0,
                                   pattern=[[-1, P]], channel_multiplier=1)
            pool.affine_select(out=upto[:, :], in_=upto[:, :], compare_op=ALU.is_ge, fill=0.0, base=0,
                               pattern=[[1, P]], channel_multiplier=-1)
            pool.affine_select(out=far_b[:, :], in_=far_b[:, :], compare_op=ALU.is_gt, fill=-FAR, base=0,
                               pattern=[[1, P]], channel_multiplier=-1)
            pool.affine_select(out=ge_tri[:, :, :], in_=ge_tri[:, :, :], compare_op=ALU.is_ge, fill=0.0, base=0,
                               pattern=[[1, E], [-1, E]], channel_multiplier=0)
            v0 = join[:, 0, :].rearrange("p (c s) -> p c s", s=2)[:, :, 1]
            pool.affine_select(out=v0, in_=v0, compare_op=ALU.not_equal, fill=-1.0, base=0,
                               pattern=[[-2, P // 2]], channel_multiplier=1)
            for k in range(1, LEVELS):
                b = 1 << k
                v = join[:, k, :].rearrange("p (c s w) -> p c s w", s=2, w=b)[:, :, 0, :]
                link(pool.memset(v, -1.0))
                link(pool.affine_select(out=v, in_=v, compare_op=ALU.is_ge, fill=0.0, base=-b,
                                        pattern=[[-2 * b, P // (2 * b)], [0, b]], channel_multiplier=1))
                last = pool.affine_select(out=v, in_=v, compare_op=ALU.is_ge, fill=0.0, base=2 * b - 1,
                                          pattern=[[2 * b, P // (2 * b)], [0, b]], channel_multiplier=-1)
            last.then_inc(consts, 1)

            pool.memset(rkT_all[:, :, 0:1], 0.0).then_inc(zero_done, 1)
            for h in range(H):
                pool.memset(S[h][:, :, :], 0.0).then_inc(zero_done, 1)

            pool.nop().then_inc(rkT_kept, H)
            with pool.Fori(0, N) as n:
                for h in range(H):
                    pool.wait_ge(rkT_sb, done(n, h))
                    pool.tensor_copy(rkT_all[:, TILES * h:TILES * h + TILES, bass.ds(n * P + 1, P)],
                                     rkTs[h][:, :, :]).then_inc(rkT_kept, 1)

            pool.wait_ge(scale_ready, 1)
            pool.partition_all_reduce(wmax[:, 4:8], wmax[:, 0:4], P, RMAX).then_inc(scale_ready, 1)
            pool.wait_ge(rkT_kept, H + N * H)

            with pool.Fori(0, N) as n:
                for h in range(H):
                    pool.wait_ge(att["x1"], n * H + (h + 1))
                    pool.tensor_copy(wkx[h][:, :, :],
                                     rkT_all[:, TILES * h:TILES * h + TILES, bass.ds(n * P, P + 1)]
                                     ).then_inc(att["wkx"], 1)
                    pool.tensor_tensor(ldU[h][:, :, :], upto[:, :].unsqueeze(1).to_broadcast([P, TILES, P]),
                                       bc(cols(sc["ld"], n, h), P), ALU.mult).then_inc(att["ldU"], 1)
                for h in range(H):
                    pool.wait_ge(att["expB"], done(n, h))
                    pool.tensor_tensor(rkd[h][:, :, :], wkx[h][:, :, 1:P + 1], expB[h][:, :, :],
                                       ALU.mult).then_inc(att["rkd"], 1)
                    pool.wait_ge(att["LT"], done(n, h))
                    pool.tensor_tensor(Tn[h][:, :, :], LT[h][:, :, :],
                                       join[:, 0, :].unsqueeze(1).to_broadcast([P, TILES, P]),
                                       ALU.mult).then_inc(att["tmp0"], 1)
                    pool.wait_ge(att["tmp0"], done(n, h))
                    pool.tensor_tensor(XT[h][:, :, :], Tn[h][:, :, :],
                                       ident[:, :].unsqueeze(1).to_broadcast([P, TILES, P]),
                                       ALU.add).then_inc(att["XT0"], 1)

        @block.scalar
        def _(act):
            small = [(wwf[:, :], W_write), (wof[:, :], W_read), (wrf[:, :], Wr), (b2_sb[:, :], b2),
                     (b1r[:, :], b1.rearrange("e (c p) -> (e c) p", p=P)),
                     (wab[:, 0:1], W_alpha.rearrange("h d -> d h")), (wab[:, 1:2], W_beta.rearrange("h d -> d h")),
                     (alog[:, :], row(A_log).to_broadcast([P, 1])), (dtb[:, :], row(dt_bias).to_broadcast([P, 1])),
                     (br_bc[:, :], row(br).to_broadcast([P, E]))]
            assert len(small) == NSMALL
            for dst, src in small:
                act.dma_start(dst, src).then_inc(small_landed, 16)

            act.wait_ge(small_landed, 16 * NSMALL)
            act.activation(nega[:, :], alog[:, :], ACT.Exp).then_inc(act_link, 1)

            act.wait_ge(wT_ps, 2)
            act.activation(WwT[:, :], bank[6][:, 0:P], ACT.Copy).then_inc(wT_sb, 1)
            act.activation(WoT[:, :], bank[6][:, P:2 * P], ACT.Copy).then_inc(wT_sb, 1)

            with act.Fori(0, N) as n:
                for h in range(H):
                    act.wait_ge(rkT_ps, H + done(n, h))
                    act.wait_ge(rkT_kept, done(n, h))
                    act.activation(rkTs[h][:, :, :], tl(h), ACT.Copy).then_inc(rkT_sb, 1)

            act.wait_ge(exp_in, 1)
            act.activation(sc["ua"][:, :], sc["na"][:, :], ACT.Exp).then_inc(act_link, 1)
            act.activation(sc["ub"][:, :], sc["nb"][:, :], ACT.Exp).then_inc(exp_out, 1)
            act.activation(sc["num"][:, :], sc["mb"][:, :], ACT.Exp).then_inc(exp_out, 1)
            act.wait_ge(act_link, 2)
            act.activation(sc["la"][:, :], sc["ua"][:, :], ACT.Ln, bias=1.0).then_inc(exp_out, 1)
            act.wait_ge(exp_in, 2)
            act.activation(sc["dexp"][:, :], sc["cum"][:, :], ACT.Exp).then_inc(exp_out, 1)
            act.activation(sc["ced"][:, :], sc["tot"][:, :], ACT.Exp).then_inc(exp_out, 1)
            act.activation(sc["tail"][:, :], sc["tmc"][:, :], ACT.Exp).then_inc(exp_out, 1)

            act.wait_ge(cols_ready, 1)
            with act.Fori(0, N) as n:
                for h in range(H):
                    b = 4 * h
                    act.wait_ge(att["x1"], n * H + (h + 1))
                    act.wait_ge(att["wkT_ps"], done(n, h))
                    for i in range(TILES):
                        ins = act.activation(wkt[h][:, i, :], tl(b)[:, i, :], ACT.Copy, scale=col(sc["tail"], n, h, i))
                    ins.then_inc(att["wkt"], 1)
                    act.wait_ge(att["B_ps"], done(n, h))
                    act.activation(expB[h][:, :, :], tl(b + 3), ACT.Exp).then_inc(att["expB"], 1)
                    act.wait_ge(att["Bm_ps"], done(n, h))
                    for i in range(TILES):
                        ins = act.activation(dec[h][:, i, :], tl(b + 3)[:, i, :], ACT.Exp, bias=col(sc["ncum"], n, h, i))
                    ins.then_inc(att["dec"], 1)
                    act.wait_ge(att["V_ps"], done(n, h))
                    for i in range(TILES):
                        ins = act.activation(V[h][:, i, :], tl(b)[:, i, :], ACT.Copy, scale=col(sc["nrm"], n, h, i))
                    ins.then_inc(att["V"], 1)
                for h in range(H):
                    act.wait_ge(att["X0_ps"], done(n, h))
                    act.activation(X[h][:, :, :], tl(4 * h), ACT.Copy).then_inc(att["X0"], 1)
                for c in range(2):
                    e = 2 * n + c
                    act.wait_ge(scale_ready, 3)
                    act.activation(w1p[:, 0, bass.ds(e, 1), :].rearrange("p a f -> p (a f)"),
                                   w1f[:, bass.ds(e, 1), :].rearrange("p a f -> p (a f)"), ACT.Copy,
                                   scale=wmax[:, 4:5]).then_inc(w_hi, 1)
                    act.activation(w2p[:, 0, bass.ds(e, 1), :, :].rearrange("p a c d -> p (a c d)"),
                                   w2f[:, bass.ds(e, 1), :, :].rearrange("p a c d -> p (a c d)"), ACT.Copy,
                                   scale=wmax[:, 5:6]).then_inc(w_hi, 1)
                for h in range(H):
                    act.wait_ge(att["VN_ps"], done(n, h))
                    for i in range(TILES):
                        ins = act.activation(vnew[h][:, i, :], tl(4 * h)[:, i, :], ACT.Copy, scale=col(sc["beta"], n, h, i))
                    ins.then_inc(att["vnew"], 1)
                for h in range(H):
                    act.wait_ge(att["OT_ps"], done(n, h))
                    act.activation(oT[h][:, :, :], tl(4 * h + 2), ACT.Copy).then_inc(att["oT"], 1)

            act.nop().then_inc(m["hhi"], 2)
            with act.Fori(0, N) as n:
                for h in range(H):
                    act.wait_ge(m["xnT_ps"], done(n, h))
                    act.activation(xp[h][:, 0, :, :], tl(0), ACT.Copy, scale=X_SCALE).then_inc(m["xhi"], 1)
                    act.wait_ge(m["lg"], done(n, h))
                    act.activation(pe_[:, :, :], lg[:, :, :], ACT.Exp).then_inc(m["e"], 1)
                    for e in range(E):
                        if e == 1:
                            act.wait_ge(m["gT_ps"], done(n, h))
                            act.activation(gT[h][:, :, :], bank[1][0:E, :].rearrange("p (t c) -> p t c", t=TILES),
                                           ACT.Copy).then_inc(m["gT"], 1)
                        for c in range(FB):
                            u = e * FB + c
                            act.wait_ge(m["up_ps"], done(n, h, E * FB, u))
                            act.wait_ge(m["hlo"], done(n, h, E * FB, u))
                            act.activation(hf[u % 2][:, :], bank[4 + u % 2][:, :], ACT.Relu,
                                           bias=b1s[:, e, c:c + 1]).then_inc(m["hf"], 1)
                            if c == 0:
                                act.wait_ge(m["dn_ps"], done(n, h, E, e))
                            act.activation(hp[e % 2][:, 0, c, :], bank[4 + u % 2][:, :], ACT.Relu,
                                           bias=b1s[:, e, c:c + 1]).then_inc(m["hhi"], 1)

        @block.vector
        def _(dve):
            count = [0]

            def link(ins):
                count[0] += 1
                ins.then_inc(dve_link, 1)
                dve.wait_ge(dve_link, count[0])

            def rsqrt(x, y, q, link):
                link(dve.tensor_scalar(y.bitcast(I32), x.bitcast(I32), -0.5, RSQRT_SEED, ALU.mult, ALU.add))
                for _ in range(3):
                    link(dve.scalar_tensor_tensor(q, y, -0.5, y, ALU.mult, ALU.mult))
                    link(dve.tensor_tensor(q, q, x, ALU.mult))
                    link(dve.scalar_tensor_tensor(y, q, 1.5, y, ALU.add, ALU.mult))

            for n in range(N):
                dve.wait_ge(x_landed[n], 16)
                for b in range(B):
                    dve.bn_stats(stats[:, n * B + b, :], x_all[:, n, b, :]).then_inc(stats_done, 1)
            dve.wait_ge(stats_done, G)
            for g in range(G):
                last = dve.bn_aggr(mv[:, g, :], stats[:, g, :])
            link(last)
            mean, var = mv[:, :, 0], mv[:, :, 1]
            link(dve.tensor_scalar(sc["ve"][:, :], var, LN_EPS, None, ALU.add))
            rsqrt(sc["ve"][:, :], sc["rstd"][:, :], sc["q"][:, :], link)
            link(dve.tensor_tensor(sc["q"][:, :], sc["rstd"][:, :], sc["rstd"][:, :], ALU.mult))
            link(dve.scalar_tensor_tensor(sc["n2"][:, :], var, float(D), sc["q"][:, :], ALU.mult, ALU.mult))
            link(dve.tensor_scalar(sc["n2"][:, :], sc["n2"][:, :], 1e-24, None, ALU.max))
            rsqrt(sc["n2"][:, :], sc["rn"][:, :], sc["q"][:, :], link)
            dve.tensor_tensor(sc["nrm"][:, :], sc["n2"][:, :], sc["rn"][:, :], ALU.mult)
            dve.tensor_scalar(sc["one"][:, :], sc["rstd"][:, :], 1.0, None, ALU.add)
            dve.tensor_tensor(sc["mr"][:, :], mean, sc["rstd"][:, :], ALU.mult)
            link(dve.tensor_tensor(sc["f"][:, :], sc["rstd"][:, :], sc["rn"][:, :], ALU.mult))

            with dve.Fori(0, N) as n:
                for h in range(H):
                    dve.wait_ge(rkT_ps, done(n, h))
                    for i in range(TILES):
                        ins = dve.tensor_scalar(rk[h][:, i, :], xg(n, h)[:, i, :],
                                                mv[:, bass.ds(n * B + (TILES * h + i), 1), 0], col(sc["f"], n, h, i),
                                                ALU.subtract, ALU.mult)
                    ins.then_inc(rk_made, 1)
                    for i in range(TILES):
                        dve.tensor_scalar(xg(n, h)[:, i, :], xg(n, h)[:, i, :], col(sc["one"], n, h, i),
                                          col(sc["mr"], n, h, i), ALU.mult, ALU.subtract).then_inc(base_ready, 1)
                    dve.wait_ge(z_ps, done(n, h))
                    dve.tensor_copy(z_all[:, bass.ds(n * B + TILES * h, TILES), :],
                                    bank[2 + h][:, 0:2 * TILES].rearrange("p (t c) -> p t c", c=2)).then_inc(z_sb, 1)

            s = {k: t[:, :] for k, t in sc.items()}
            dve.wait_ge(z_sb, N * H)
            dve.wait_ge(small_landed, 16 * NSMALL)
            link(dve.tensor_tensor(s["za"], z_all[:, :, 0], s["nrm"], ALU.mult))
            link(dve.tensor_tensor(s["zb"], z_all[:, :, 1], s["nrm"], ALU.mult))
            link(dve.tensor_scalar(s["za"], s["za"], dtb[:, :], None, ALU.add))
            link(dve.scalar_tensor_tensor(s["na"], s["za"], -1.0, s["za"], ALU.mult, ALU.min))
            link(dve.scalar_tensor_tensor(s["nb"], s["zb"], -1.0, s["zb"], ALU.mult, ALU.min))
            dve.tensor_scalar(s["mb"], s["zb"], 0.0, None, ALU.min).then_inc(exp_in, 1)
            dve.wait_ge(exp_out, 3)
            link(dve.scalar_tensor_tensor(s["la"], s["za"], 0.0, s["la"], ALU.max, ALU.add))
            dve.wait_ge(act_link, 1)
            link(dve.tensor_scalar(nega[:, :], nega[:, :], -1.0, None, ALU.mult))
            dve.tensor_scalar(s["ld"], s["la"], nega[:, :], None, ALU.mult).then_inc(ld_ready, 1)
            link(dve.tensor_scalar(s["den"], s["ub"], 1.0, None, ALU.add))
            link(dve.reciprocal(s["den"], s["den"]))
            link(dve.tensor_tensor(s["beta"], s["den"], s["num"], ALU.mult))
            dve.wait_ge(cum_ps, 2)
            link(dve.tensor_copy(s["cum"], bank[0][:, 0:G]))
            link(dve.tensor_copy(s["tot"], bank[0][:, G:2 * G]))
            link(dve.tensor_scalar(s["ncum"], s["cum"], -1.0, None, ALU.mult))
            dve.tensor_tensor(s["tmc"], s["tot"], s["cum"], ALU.subtract).then_inc(exp_in, 1)

            dve.wait_ge(w1_landed, 16)
            dve.wait_ge(w2_landed, 16 * E)
            dve.wait_ge(b1T_ps, 1)
            for k, t in enumerate((w1f[:, :, :].rearrange("p e f -> p (e f)"),
                                   w2f[:, :, :, :].rearrange("p e c d -> p (e c d)"), wrf[:, :],
                                   bank[7][:, 0:E * FB])):
                last = dve.tensor_reduce(wmax[:, k:k + 1], t, AX_X, ALU.max, apply_absolute_value=True)
            last.then_inc(scale_ready, 1)
            dve.wait_ge(exp_out, 6)
            dve.tensor_scalar(s["ndexp"], s["dexp"], -1.0, None, ALU.mult).then_inc(cols_ready, 1)

            dve.wait_ge(scale_ready, 2)
            link(dve.scalar_tensor_tensor(wmax[:, 4:5], wmax[:, 4:5], float(P), wmax[:, 7:8], ALU.mult, ALU.add))
            link(dve.tensor_scalar(wmax[:, 4:7], wmax[:, 4:7], 1e-30, None, ALU.max))
            link(dve.tensor_scalar(wmax[:, 4:7].bitcast(I32), wmax[:, 4:7].bitcast(I32), 0x7F800000, None, ALU.bitwise_and))
            link(dve.reciprocal(wmax[:, 4:7], wmax[:, 4:7]))
            link(dve.tensor_scalar(wmax[:, 4:5], wmax[:, 4:5], 2.0 ** 14 / X_SCALE, None, ALU.mult))
            link(dve.tensor_scalar(wmax[:, 5:7], wmax[:, 5:7], 2.0 ** 12, None, ALU.mult))
            link(dve.tensor_scalar(wmax[:, 0:1], wmax[:, 6:7], X_SCALE, None, ALU.mult))
            link(dve.scalar_tensor_tensor(wmax[:, 1:2], wmax[:, 4:5], X_SCALE, wmax[:, 5:6], ALU.mult, ALU.mult))
            link(dve.reciprocal(wmax[:, 0:2], wmax[:, 0:2]))
            link(dve.tensor_scalar(b1s[:, :, :].rearrange("p e c -> p (e c)"), bank[7][:, 0:E * FB], wmax[:, 4:5], X_SCALE,
                                   ALU.mult, ALU.mult))
            link(dve.tensor_scalar(wrp[:, 0, :], wrf[:, :], wmax[:, 6:7], None, ALU.mult))
            link(dve.scalar_tensor_tensor(wrp[:, 1, :], wrf[:, :], wmax[:, 6:7], wrp[:, 0, :], ALU.mult, ALU.subtract))
            dve.nop().then_inc(scale_ready, 1)

            dve.wait_ge(zero_done, 1 + H)
            dve.wait_ge(base_ready, G)
            dve.nop().then_inc(att["S"], H)
            dve.nop().then_inc(att["x1"], H)
            with dve.Fori(0, N) as n:
                for h in range(H):
                    b = 4 * h
                    dve.wait_ge(att["gq_ps"], done(n, h))
                    dve.wait_ge(att["dec"], done(n, h))
                    for i in range(TILES):
                        ins = dve.scalar_tensor_tensor(LT[h][:, i, :], gq(h)[i // 2][:, i % 2, 0:P], col(sc["beta"], n, h, i),
                                                       dec[h][:, i, :], ALU.mult, ALU.mult)
                    ins.then_inc(att["LT"], 1)
                    for c in range(2):
                        ins = dve.tensor_tensor(intraT[h][:, 2 * c:2 * c + 2, :], gq(h)[c][:, :, 1:P + 1],
                                                dec[h][:, 2 * c:2 * c + 2, :], ALU.mult)
                    ins.then_inc(att["intra"], 1)
                    dve.wait_ge(att["WS_ps"], done(n, h))
                    dve.wait_ge(att["V"], done(n, h))
                    for i in range(TILES):
                        ins = dve.scalar_tensor_tensor(R[h][:, i, :], tl(b + 3)[:, i, :], col(sc["ndexp"], n, h, i),
                                                       V[h][:, i, :], ALU.mult, ALU.add)
                    ins.then_inc(att["R"], 1)
                for k in range(1, LEVELS):
                    for h in range(H):
                        b = 4 * h
                        dve.wait_ge(att["T_ps"], lev(n, h, k - 1, LEVELS - 1))
                        dve.tensor_tensor(Tn[h][:, :, :], tl(b), join[:, k, :].unsqueeze(1).to_broadcast([P, TILES, P]),
                                          ALU.mult).then_inc(att["Tn"], 1)
                    for h in range(H):
                        b = 4 * h
                        if k < LEVELS - 1:
                            dve.wait_ge(att["XC_ps"], lev(n, h, k - 1, LEVELS - 2))
                            dve.tensor_tensor(X[h][:, :, :], tl(b + 1), X[h][:, :, :], ALU.add).then_inc(att["X"], 1)
                        dve.wait_ge(att["XTC_ps"], lev(n, h, k - 1, LEVELS - 1))
                        dve.tensor_tensor(XT[h][:, :, :], tl(b + 2), XT[h][:, :, :], ALU.add).then_inc(att["XT"], 1)
                for c in range(2):
                    e = 2 * n + c
                    for k, (wf, wp) in enumerate(((w1f[:, bass.ds(e, 1), :].rearrange("p a f -> p (a f)"),
                                                   [w1p[:, q, bass.ds(e, 1), :].rearrange("p a f -> p (a f)") for q in range(2)]),
                                                  (w2f[:, bass.ds(e, 1), :, :].rearrange("p a c d -> p (a c d)"),
                                                   [w2p[:, q, bass.ds(e, 1), :, :].rearrange("p a c d -> p (a c d)") for q in range(2)]))):
                        dve.wait_ge(w_hi, n * 4 + (2 * c + k + 1))
                        dve.scalar_tensor_tensor(wp[1], wf, wmax[:, 4 + k:5 + k], wp[0], ALU.mult,
                                                 ALU.subtract).then_inc(w_lo, 1)
                for h in range(H):
                    b = 4 * h
                    dve.wait_ge(att["SN_ps"], done(n, h))
                    dve.wait_ge(att["OT_ps"], done(n, h))
                    for i in range(TILES):
                        ins = dve.scalar_tensor_tensor(S[h][:, i, :], S[h][:, i, :], col(sc["ced"], n, h, i),
                                                       tl(b + 1)[:, i, :], ALU.mult, ALU.add)
                    ins.then_inc(att["S"], 1)
                for h in range(H):
                    b = 4 * h
                    dve.wait_ge(att["O_ps"], done(n, h))
                    dve.tensor_tensor(xg(n, h), tl(b + 3), xg(n, h), ALU.add).then_inc(att["x1"], 1)

            dve.wait_ge(att["x1"], H + N * H)
            dve.nop().then_inc(m["hlo"], 2)
            LINKS = 34
            with dve.Fori(0, N) as n:
                for h in range(H):
                    cnt = [0]

                    def mlink(ins):
                        cnt[0] += 1
                        ins.then_inc(m["link"], 1)
                        dve.wait_ge(m["link"], n * (H * LINKS) + (h * LINKS + cnt[0]))

                    for i in range(TILES):
                        last = dve.bn_stats(mst[:, i, :], xg(n, h)[:, i, :])
                    mlink(last)
                    dve.sem_inc(m["link"], 1)
                    cnt[0] += 1
                    for i in range(TILES):
                        last = dve.bn_aggr(mmv[:, i, :], mst[:, i, :])
                    mlink(last)
                    r = {k: t[:, :] for k, t in mr_.items()}
                    mlink(dve.tensor_scalar(r["ve"], mmv[:, :, 1], LN_EPS, None, ALU.add))
                    rsqrt(r["ve"], r["r"], r["q"], mlink)
                    for i in range(TILES):
                        last = dve.tensor_scalar(xn[h][:, i, :], xg(n, h)[:, i, :], mmv[:, i, 0:1], mr_["r"][:, i:i + 1],
                                                 ALU.subtract, ALU.mult)
                    last.then_inc(m["xn"], 1)
                    dve.wait_ge(m["xhi"], done(n, h))
                    dve.scalar_tensor_tensor(xp[h][:, 1, :, :], tl(0), X_SCALE, xp[h][:, 0, :, :], ALU.mult,
                                             ALU.subtract).then_inc(m["xlo"], 1)
                    dve.wait_ge(m["lg_ps"], done(n, h))
                    mlink(dve.scalar_tensor_tensor(lg[:, :, :], bank[2][:, 0:TILES * E].rearrange("p (t e) -> p t e", e=E),
                                                   wmax[:, 0:1], br_bc[:, :].unsqueeze(1).to_broadcast([P, TILES, E]),
                                                   ALU.mult, ALU.add))
                    mlink(dve.tensor_reduce(r["mx"], lg[:, :, :], AX_X, ALU.max))
                    dve.tensor_tensor(lg[:, :, :], lg[:, :, :], bc(r["mx"], E), ALU.subtract).then_inc(m["lg"], 1)
                    dve.wait_ge(m["e"], done(n, h))
                    mlink(dve.tensor_reduce(r["sum"], pe_[:, :, :], AX_X, ALU.add))
                    mlink(dve.reciprocal(r["rs"], r["sum"]))
                    mlink(dve.tensor_tensor(pr[:, :, :], pe_[:, :, :], bc(r["rs"], E), ALU.mult))
                    pj = pr[:, :, :].unsqueeze(2).to_broadcast([P, TILES, E, E])
                    pe = pr[:, :, :].unsqueeze(3).to_broadcast([P, TILES, E, E])
                    tri = ge_tri[:, :, :].unsqueeze(1).to_broadcast([P, TILES, E, E])
                    mlink(dve.tensor_tensor(cmp1[:, :, :, :], pj, pe, ALU.is_ge))
                    mlink(dve.tensor_tensor(cmp2[:, :, :, :], pj, pe, ALU.is_gt))
                    mlink(dve.tensor_tensor(cmp1[:, :, :, :], cmp1[:, :, :, :], tri, ALU.mult))
                    mlink(dve.tensor_tensor(cmp1[:, :, :, :], cmp1[:, :, :, :], cmp2[:, :, :, :], ALU.max))
                    mlink(dve.tensor_tensor(cmp1[:, :, :, :], cmp1[:, :, :, :], pj, ALU.mult))
                    mlink(dve.tensor_reduce(cumt[:, :, :], cmp1[:, :, :, :], AX_X, ALU.add))
                    mlink(dve.tensor_scalar(k1[:, :, :], cumt[:, :, :], TOP_P, None, ALU.is_lt))
                    mlink(dve.tensor_tensor(k2[:, :, :], cumt[:, :, :], pr[:, :, :], ALU.is_le))
                    mlink(dve.tensor_tensor(k1[:, :, :], k1[:, :, :], k2[:, :, :], ALU.max))
                    dve.tensor_tensor(gate[h][:, :, :], pr[:, :, :], k1[:, :, :], ALU.mult).then_inc(m["gate"], 1)
                    dve.wait_ge(m["gate"], done(n, h))
                    mlink(dve.tensor_scalar(gates[h][:, :, :], gate[h][:, :, :], wmax[:, 1:2], None, ALU.mult))
                    assert cnt[0] <= LINKS, cnt
                    if cnt[0] < LINKS:
                        dve.nop().then_inc(m["link"], LINKS - cnt[0])

                    def gather(e):
                        dve.wait_ge(m["dn_ps"], 2 + n * (H * E) + (h * E + e + 1))
                        for i in range(TILES):
                            ins = dve.scalar_tensor_tensor(xg(n, h)[:, i, :], tl(6 + e % 2)[:, i, :], gates[h][:, i, e:e + 1],
                                                           xg(n, h)[:, i, :], ALU.mult, ALU.add)
                        ins.then_inc(m["acc"], 1)
                        dve.wait_ge(m["acc"], done(n, h, E, e))

                    for e in range(E):
                        if e == 1:
                            dve.wait_ge(m["b2_ps"], done(n, h))
                            dve.tensor_tensor(xg(n, h), tl(3), xg(n, h), ALU.add).then_inc(m["acc0"], 1)
                            dve.wait_ge(m["acc0"], done(n, h))
                        for c in range(FB):
                            u = e * FB + c
                            dve.wait_ge(m["hf"], done(n, h, E * FB, u))
                            dve.wait_ge(m["hhi"], 2 + done(n, h, E * FB, u))
                            dve.tensor_tensor(hp[e % 2][:, 1, c, :], hf[u % 2][:, :], hp[e % 2][:, 0, c, :],
                                              ALU.subtract).then_inc(m["hlo"], 1)
                        if e >= 1:
                            gather(e - 1)
                    gather(E - 1)

        @block.tensor
        def _(pe):
            pe.wait_ge(consts, 1)
            pe.wait_ge(small_landed, 16 * NSMALL)
            pe.transpose(bank[6][:, 0:P], wwf[:, :], ident[:, :]).then_inc(wT_ps, 1)
            pe.transpose(bank[6][:, P:2 * P], wof[:, :], ident[:, :]).then_inc(wT_ps, 1)
            pe.transpose(bank[7][:, 0:E * FB], b1r[:, :], ident[0:E * FB, 0:E * FB]).then_inc(b1T_ps, 1)

            pe.nop().then_inc(rkT_ps, H)
            with pe.Fori(0, N) as n:
                for h in range(H):
                    pe.wait_ge(rk_made, done(n, h))
                    for i in range(TILES):
                        ins = pe.transpose(tl(h)[:, i, :], rk[h][:, i, :], ident[:, :])
                    ins.then_inc(rkT_ps, 1)
                    pe.wait_ge(rkT_sb, done(n, h))
                    for i in range(TILES):
                        ins = pe.matmul(bank[2 + h][:, 2 * i:2 * i + 2], rkTs[h][:, i, :], wab[:, :], start=True, stop=True)
                    ins.then_inc(z_ps, 1)

            pe.wait_ge(ld_ready, 1)
            pe.matmul(bank[0][:, 0:G], upto[:, :], sc["ld"][:, :], start=True, stop=True).then_inc(cum_ps, 1)
            pe.matmul(bank[0][:, G:2 * G], ones[:, :], sc["ld"][:, :], start=True, stop=True).then_inc(cum_ps, 1)

            pe.wait_ge(wT_sb, 2)
            pe.wait_ge(cols_ready, 1)
            with pe.Fori(0, N) as n:
                for h in range(H):
                    b = 4 * h
                    pe.wait_ge(att["x1"], n * H + (h + 1))
                    pe.wait_ge(att["wkx"], done(n, h))
                    for i in range(TILES):
                        ins = pe.transpose(tl(b)[:, i, :], wkx[h][:, i, 0:P], ident[:, :])
                    ins.then_inc(att["wkT_ps"], 1)
                    for i in range(TILES):
                        ins = pe.matmul(gq(h)[i // 2][:, i % 2, :], wkx[h][:, i, 0:P], wkx[h][:, i, :], start=True, stop=True)
                    ins.then_inc(att["gq_ps"], 1)
                    pe.wait_ge(att["ldU"], done(n, h))
                    pe.matmul(bank[b + 3][:, :], ones[:, :], ldU[h][:, :, :].rearrange("p t c -> p (t c)"), start=True,
                              stop=False, skip_group_check=True).then_inc(att["B_ps"], 1)
                    pe.wait_ge(att["wkt"], done(n, h))
                    for i in range(TILES):
                        ins = pe.matmul(tl(b)[:, i, :], wkx[h][:, i, 1:P + 1], WwT[:, :], start=True, stop=True)
                    ins.then_inc(att["V_ps"], 1)
                    pe.wait_ge(att["expB"], done(n, h))
                    pe.matmul(bank[b + 3][:, :], ident_b[:, :], far_b[:, :].unsqueeze(1).to_broadcast([P, TILES, P]),
                              start=False, stop=True, skip_group_check=True).then_inc(att["Bm_ps"], 1)
                    pe.wait_ge(att["dec"], done(n, h))
                    pe.wait_ge(att["S"], n * H + (h + 1))
                    for i in range(TILES):
                        ins = pe.matmul(tl(b + 3)[:, i, :], wkx[h][:, i, 0:P], S[h][:, i, :], start=True, stop=True)
                    ins.then_inc(att["WS_ps"], 1)
                for h in range(H):
                    pe.wait_ge(att["XT0"], done(n, h))
                    pe.wait_ge(att["V"], done(n, h))
                    for i in range(TILES):
                        ins = pe.transpose(tl(4 * h)[:, i, :], XT[h][:, i, :], ident[:, :])
                    ins.then_inc(att["X0_ps"], 1)
                for k in range(1, LEVELS):
                    for h in range(H):
                        b = 4 * h
                        if k == 1:
                            pe.wait_ge(att["X0"], done(n, h))
                        else:
                            pe.wait_ge(att["X"], lev(n, h, k - 2, LEVELS - 2))
                        for i in range(TILES):
                            ins = pe.matmul(tl(b)[:, i, :], LT[h][:, i, :], X[h][:, i, :], start=True, stop=True)
                        ins.then_inc(att["T_ps"], 1)
                    for h in range(H):
                        b = 4 * h
                        pe.wait_ge(att["Tn"], lev(n, h, k - 1, LEVELS - 1))
                        if k == 1:
                            pe.wait_ge(att["intra"], done(n, h))
                        else:
                            pe.wait_ge(att["XT"], lev(n, h, k - 2, LEVELS - 1))
                        if k < LEVELS - 1:
                            for i in range(TILES):
                                ins = pe.matmul(tl(b + 1)[:, i, :], XT[h][:, i, :], Tn[h][:, i, :], start=True, stop=True)
                            ins.then_inc(att["XC_ps"], 1)
                        for i in range(TILES):
                            ins = pe.matmul(tl(b + 2)[:, i, :], Tn[h][:, i, :], XT[h][:, i, :], start=True, stop=True)
                        ins.then_inc(att["XTC_ps"], 1)
                for h in range(H):
                    b = 4 * h
                    pe.wait_ge(att["XT"], lev(n, h, LEVELS - 2, LEVELS - 1))
                    pe.wait_ge(att["R"], done(n, h))
                    for i in range(TILES):
                        ins = pe.matmul(tl(b)[:, i, :], XT[h][:, i, :], R[h][:, i, :], start=True, stop=True)
                    ins.then_inc(att["VN_ps"], 1)
                for h in range(H):
                    b = 4 * h
                    pe.wait_ge(att["vnew"], done(n, h))
                    pe.wait_ge(att["rkd"], done(n, h))
                    for i in range(TILES):
                        ins = pe.matmul(tl(b + 1)[:, i, :], wkt[h][:, i, :], vnew[h][:, i, :], start=True, stop=True)
                    ins.then_inc(att["SN_ps"], 1)
                    for i in range(TILES):
                        pe.matmul(tl(b + 2)[:, i, :], S[h][:, i, :], rkd[h][:, i, :], start=True, stop=False)
                        ins = pe.matmul(tl(b + 2)[:, i, :], vnew[h][:, i, :], intraT[h][:, i, :], start=False, stop=True)
                    ins.then_inc(att["OT_ps"], 1)
                for h in range(H):
                    b = 4 * h
                    pe.wait_ge(att["oT"], done(n, h))
                    for i in range(TILES):
                        ins = pe.matmul(tl(b + 3)[:, i, :], oT[h][:, i, :], WoT[:, :], start=True, stop=True)
                    ins.then_inc(att["O_ps"], 1)

            pe.wait_ge(w_lo, 2 * E)
            pe.nop().then_inc(m["dn_ps"], 2)
            with pe.Fori(0, N) as n:
                for h in range(H):
                    pe.wait_ge(m["xn"], done(n, h))
                    for i in range(TILES):
                        ins = pe.transpose(tl(0)[:, i, :], xn[h][:, i, :], ident[:, :])
                    ins.then_inc(m["xnT_ps"], 1)
                    pe.wait_ge(m["xlo"], done(n, h))
                    for i in range(TILES):
                        for a in range(2):
                            for w in range(2):
                                ins = pe.matmul(bank[2][:, E * i:E * i + E], xp[h][:, a, i, :], wrp[:, w, :],
                                                start=(a == 0 and w == 0), stop=(a == 1 and w == 1))
                    ins.then_inc(m["lg_ps"], 1)

                    def up(e):
                        for c in range(FB):
                            u = e * FB + c
                            pe.wait_ge(m["hhi"], done(n, h, E * FB, u))
                            for j, (a, w) in enumerate(((0, 0), (1, 0), (0, 1))):
                                ins = pe.matmul(bank[4 + u % 2][:, :], w1p[:, w, e, c * P:(c + 1) * P],
                                                xp[h][:, a, :, :].rearrange("p t c -> p (t c)"), start=(j == 0), stop=(j == 2))
                            ins.then_inc(m["up_ps"], 1)

                    def down(e):
                        pe.wait_ge(m["hlo"], 2 + n * (H * E * FB) + (h * E * FB + e * FB + FB))
                        if e >= 2:
                            pe.wait_ge(m["acc"], done(n, h, E, e - 2))
                        for i in range(TILES):
                            for c in range(FB):
                                for j, (a, w) in enumerate(((0, 0), (0, 1), (1, 0))):
                                    ins = pe.matmul(tl(6 + e % 2)[:, i, :], hp[e % 2][:, a, c, i * P:(i + 1) * P],
                                                    w2p[:, w, e, c, :], start=(c == 0 and j == 0),
                                                    stop=(c == FB - 1 and j == 2))
                        ins.then_inc(m["dn_ps"], 1)

                    up(0)
                    pe.wait_ge(m["gate"], done(n, h))
                    for i in range(TILES):
                        ins = pe.transpose(bank[1][0:E, i * P:(i + 1) * P], gate[h][:, i, :], ident[:, :])
                    ins.then_inc(m["gT_ps"], 1)
                    up(1)
                    pe.wait_ge(m["gT"], done(n, h))
                    for i in range(TILES):
                        ins = pe.matmul(tl(3)[:, i, :], gT[h][:, i, :], b2_sb[:, :], start=True, stop=True)
                    ins.then_inc(m["b2_ps"], 1)
                    down(0)
                    for e in range(2, E):
                        up(e)
                        down(e - 1)
                    down(E - 1)


_INS = ['L0_attn_out', 'L0_attn_W_write', 'L0_attn_W_read', 'L0_attn_W_alpha', 'L0_attn_W_beta', 'L0_attn_A_log',
        'L0_attn_dt_bias', 'L0_ffn_Wr', 'L0_ffn_br', 'L0_ffn_W1', 'L0_ffn_b1', 'L0_ffn_W2', 'L0_ffn_b2']


def kernel(**inputs):
    import numpy as _np
    import concourse.bacc as _bacc
    from concourse import mybir as _mybir
    from concourse.bass_utils import run_bass_kernel_spmd as _run

    nc = _bacc.Bacc("TRN2", target_bir_lowering=False, num_devices=1)
    arrays, args = {}, []
    for name in _INS:
        a = _np.ascontiguousarray(inputs[name])
        arrays[f"in_{name}_dram"] = a
        args.append(nc.dram_tensor(f"in_{name}_dram", a.shape, _mybir.dt.from_np(a.dtype), kind="ExternalInput").ap())
    x = inputs['L0_attn_out']
    args.append(nc.dram_tensor("out_0_dram", x.shape, _mybir.dt.float32, kind="ExternalOutput").ap())
    preln_layer(nc, *args)
    r = _run(nc, [arrays], core_ids=[0])
    return r.results[0]["out_0_dram"]
```

```python
from contextlib import ExitStack

import concourse.bass as bass
from concourse import mybir

P = 128
TILES = 4
LEVELS = 7
LN_EPS = 1e-5
TOP_P = 0.8
X_SCALE = 16.0
FAR = 1e30
RSQRT_SEED = float(0x5F3759DF)

ALU = mybir.AluOpType
ACT = mybir.ActivationFunctionType
AX_X = mybir.AxisListType.X
F32 = mybir.dt.float32
F16 = mybir.dt.float16
BF16 = mybir.dt.bfloat16
I32 = mybir.dt.int32
RMAX = bass.bass_isa.ReduceOp.max


def preln_layer(nc, x_in, W_write, W_read, W_alpha, W_beta, A_log, dt_bias, Wr, br, W1, b1, W2, b2, out):
    B, T, D = x_in.shape
    E, _, F = W1.shape
    N = T // P
    H = B // TILES
    G = N * B
    FB = F // P
    assert D == P and TILES * P == 512 and B == H * TILES and H == 2 and E == 8

    x_v = x_in.rearrange("b (n p) d -> n p b d", p=P)
    out_v = out.rearrange("b (n p) d -> p n b d", p=P)
    row = lambda v: v.rearrange("(a n) -> a n", a=1)

    ctx = ExitStack()
    with ctx:
        def sb(name, shape, dt=F32):
            return ctx.enter_context(nc.sbuf_tensor(name, shape, dt))

        def sem(name):
            return ctx.enter_context(nc.semaphore(name))

        x_all = sb("x_all", [P, N, B, D])
        rkT_all = sb("rkT_all", [P, B, 1 + T])
        w1f = sb("w1f", [P, E, F])
        w2f = sb("w2f", [P, E, FB, D])
        w1p = sb("w1p", [P, 2, E, F], F16)
        w2p = sb("w2p", [P, 2, E, FB, D], F16)
        wrf = sb("wrf", [P, E])
        wrp = sb("wrp", [P, 2, E], F16)
        wwf = sb("wwf", [P, D])
        wof = sb("wof", [P, D])
        WwT = sb("WwT", [P, D])
        WoT = sb("WoT", [P, D])
        wab = sb("wab", [P, 2])
        alog = sb("alog", [P, 1])
        dtb = sb("dtb", [P, 1])
        nega = sb("nega", [P, 1])
        br_bc = sb("br_bc", [P, E])
        b2_sb = sb("b2_sb", [E, D])
        b1r = sb("b1r", [E * FB, P])
        b1s = sb("b1s", [P, E, FB])

        ident = sb("ident", [P, P])
        ident_b = sb("ident_b", [P, P], BF16)
        ones = sb("ones", [P, P])
        ones_b = sb("ones_b", [P, P], BF16)
        after = sb("after", [P, P])
        after_b = sb("after_b", [P, P], BF16)
        upto = sb("upto", [P, P])
        far_b = sb("far_b", [P, P], BF16)
        join = sb("join", [P, LEVELS, P])
        ge_tri = sb("ge_tri", [P, E, E])

        stats = sb("stats", [P, G, 6])
        mv = sb("mv", [P, G, 2])
        sc = {k: sb("sc_" + k, [P, G]) for k in
              ("ve", "rstd", "q", "n2", "rn", "nrm", "f", "one", "mr", "za", "zb", "na", "nb", "ua", "ub",
               "la", "den", "mb", "num", "ld", "ldr", "dexp", "ndexp", "ced", "tail", "beta")}
        ldp = sb("ldp", [P, 3, G], BF16)
        z_all = sb("z_all", [P, G, 2])
        wmax = sb("wmax", [P, 8])

        rk = [sb(f"rk{h}", [P, TILES, D]) for h in range(H)]
        rkTs = [sb(f"rkTs{h}", [P, TILES, P]) for h in range(H)]
        wkx = [sb(f"wkx{h}", [P, TILES, P + 1]) for h in range(H)]
        ldU = [sb(f"ldU{h}", [P, 3, TILES, P], BF16) for h in range(H)]
        wkt = [sb(f"wkt{h}", [P, TILES, D]) for h in range(H)]
        expB = [sb(f"expB{h}", [P, TILES, P]) for h in range(H)]
        dec = [sb(f"dec{h}", [P, TILES, P]) for h in range(H)]
        rkd = [sb(f"rkd{h}", [P, TILES, P]) for h in range(H)]
        V = [sb(f"V{h}", [P, TILES, D]) for h in range(H)]
        LT = [sb(f"LT{h}", [P, TILES, P]) for h in range(H)]
        intraT = [sb(f"intraT{h}", [P, TILES, P]) for h in range(H)]
        X = [sb(f"X{h}", [P, TILES, P]) for h in range(H)]
        XT = [sb(f"XT{h}", [P, TILES, P]) for h in range(H)]
        Tn = [sb(f"Tn{h}", [P, TILES, P]) for h in range(H)]
        R = [sb(f"R{h}", [P, TILES, D]) for h in range(H)]
        vnew = [sb(f"vnew{h}", [P, TILES, D]) for h in range(H)]
        oT = [sb(f"oT{h}", [P, TILES, P]) for h in range(H)]
        S = [sb(f"S{h}", [P, TILES, D]) for h in range(H)]

        xn = rk
        xp = [sb(f"xp{h}", [P, 2, TILES, P], F16) for h in range(H)]
        w2words = w2f[:, :, :, :].rearrange("p e c d -> p (e c d)")
        hf = [w2words[:, 512 * i:512 * (i + 1)] for i in range(2)]
        hp = [w1f[:, E // 2 * i:E // 2 * (i + 1), :].rearrange("p e f -> p (e f)").bitcast(F16).rearrange(
            "p (a c t) -> p a c t", a=2, c=FB) for i in range(2)]
        mst = sb("mst", [P, TILES, 6])
        mmv = sb("mmv", [P, TILES, 2])
        mr_ = {k: sb("m_" + k, [P, TILES]) for k in ("ve", "r", "q", "mx", "sum", "rs")}
        lg = sb("lg", [P, TILES, E])
        pe_ = sb("pe_", [P, TILES, E])
        pr = sb("pr", [P, TILES, E])
        cmp1 = sb("cmp1", [P, TILES, E, E])
        cmp2 = sb("cmp2", [P, TILES, E, E])
        cumt = sb("cumt", [P, TILES, E])
        k1 = sb("k1", [P, TILES, E])
        k2 = sb("k2", [P, TILES, E])
        gate = [sb(f"gate{h}", [P, TILES, E]) for h in range(H)]
        gates = [sb(f"gates{h}", [P, TILES, E]) for h in range(H)]
        gT = [sb(f"gT{h}", [E, TILES, P]) for h in range(H)]

        bank = [ctx.enter_context(nc.psum_tensor(f"bank{i}", [P, 512], F32)) for i in range(8)]
        tl = lambda b: bank[b][:, :].rearrange("p (t c) -> p t c", t=TILES)

        def gq(bk):
            return [bank[b][:, 0:2 * (P + 1)].rearrange("p (t c) -> p t c", t=2) for b in bk[1:3]]

        ATT = (0, 1, 2)
        ATT_FIRST = ((0, 1, 2), (4, 5, 6))
        PREP, UP, DOWN = 3, (4, 5), (6, 7)

        x_landed = [sem(f"x_landed{n}") for n in range(N)]
        small_landed = sem("small_landed")
        w1_landed, w2_landed = sem("w1_landed"), sem("w2_landed")
        consts = sem("consts")
        pool_link, dve_link, act_link = sem("pool_link"), sem("dve_link"), sem("act_link")
        zero_done = sem("zero_done")
        wT_ps, wT_sb = sem("wT_ps"), sem("wT_sb")
        b1T_ps = sem("b1T_ps")
        wr_hi = sem("wr_hi")
        stats_done = sem("stats_done")
        rk_made, rkT_ps, rkT_sb, rkT_kept, z_ps, z_sb = (sem(s) for s in ("rk_made", "rkT_ps", "rkT_sb", "rkT_kept", "z_ps", "z_sb"))
        exp_in, exp_out = sem("exp_in"), sem("exp_out")
        ld_ready, cum_ps, cols_ready = sem("ld_ready"), sem("cum_ps"), sem("cols_ready")
        base_ready = sem("base_ready")
        scale_ready = sem("scale_ready")
        att = [{k: sem(f"att{h}_{k}") for k in
                ("wkx", "ldU", "wkT_ps", "wkt", "gq_ps", "B_ps", "expB", "D_ps", "dec", "rkd", "V_ps", "V", "WS_ps",
                 "R", "LT", "intra", "tmp0", "XT0", "X0_ps", "X0", "T_ps", "Tn", "XC_ps", "X", "turn_ps", "XT",
                 "last_ps", "A", "VN_ps", "vnew", "SN_ps", "S", "OT_ps", "oT", "O_ps", "x1")} for h in range(H)]
        w_hi, w_lo = sem("w_hi"), sem("w_lo")
        m = {k: sem("moe_" + k) for k in
             ("link", "xn", "xnT_ps", "xhi", "xlo", "lg_ps", "lg", "e", "gate", "gT_ps", "gT", "b2_ps", "acc0",
              "up_ps", "hf", "hhi", "hlo", "dn_ps", "acc", "stored")}

        block = ctx.enter_context(nc.Block())

        def done(n, h, per=1, k=0):
            return n * (H * per) + (h * per + k + 1)

        def nth(n, per=1, k=0):
            return n * per + (k + 1)

        col = lambda t, n, h, i: t[:, bass.ds(n * B + (TILES * h + i), 1)]
        cols = lambda t, n, h: t[:, bass.ds(n * B + TILES * h, TILES)]
        bc = lambda a, w: a.unsqueeze(2).to_broadcast([P, TILES, w])
        xg = lambda n, h: x_all[:, bass.ds(n, 1), TILES * h:TILES * h + TILES, :].rearrange("p a b d -> p (a b) d")

        NSMALL = 10
        UNITS = E * FB
        T_AT = [6 + 2 * k for k in range(1, LEVELS)]
        TURN_AT = [t + 2 for t in T_AT[:-1]]

        @block.sync
        def _(sp):
            for n in range(N):
                sp.dma_start(x_all[:, n, :, :], x_v[n]).then_inc(x_landed[n], 16)
            sp.dma_start(w1f[:, :, :], W1.rearrange("e h f -> h e f")).then_inc(w1_landed, 16)
            for e in range(E):
                sp.dma_start(w2f[:, e, :, :], W2[e].rearrange("(c p) h -> p c h", p=P)).then_inc(w2_landed, 16)
            with sp.Fori(0, N) as n:
                for h in range(H):
                    sp.wait_ge(m["acc"], 2 + done(n, h, E, E - 1))
                    sp.dma_start(out_v[:, bass.ds(n, 1), TILES * h:TILES * h + TILES, :].rearrange("p a b d -> p (a b) d"),
                                 xg(n, h)).then_inc(m["stored"], 16)
            sp.wait_ge(m["stored"], 16 * N * H)

        @block.gpsimd
        def _(pool):
            count = [0]

            def link(ins):
                count[0] += 1
                ins.then_inc(pool_link, 1)
                pool.wait_ge(pool_link, count[0])

            pool.memset(ones[:, :], 1.0)
            pool.memset(ones_b[:, :], 1.0)
            pool.memset(after[:, :], 1.0)
            pool.memset(after_b[:, :], 1.0)
            pool.memset(ident[:, :], 0.0)
            pool.memset(ident_b[:, :], 0.0)
            pool.memset(far_b[:, :], 0.0)
            pool.memset(upto[:, :], 1.0)
            pool.memset(ge_tri[:, :, :], 1.0)
            link(pool.memset(join[:, :, :], 0.0))
            for t in (ident, ident_b):
                pool.affine_select(out=t[:, :], in_=t[:, :], compare_op=ALU.not_equal, fill=1.0, base=0,
                                   pattern=[[-1, P]], channel_multiplier=1)
            pool.affine_select(out=upto[:, :], in_=upto[:, :], compare_op=ALU.is_ge, fill=0.0, base=0,
                               pattern=[[1, P]], channel_multiplier=-1)
            for t in (after, after_b):
                pool.affine_select(out=t[:, :], in_=t[:, :], compare_op=ALU.is_gt, fill=0.0, base=0,
                                   pattern=[[-1, P]], channel_multiplier=1)
            pool.affine_select(out=far_b[:, :], in_=far_b[:, :], compare_op=ALU.is_gt, fill=-FAR, base=0,
                               pattern=[[1, P]], channel_multiplier=-1)
            pool.affine_select(out=ge_tri[:, :, :], in_=ge_tri[:, :, :], compare_op=ALU.is_ge, fill=0.0, base=0,
                               pattern=[[1, E], [-1, E]], channel_multiplier=0)
            v0 = join[:, 0, :].rearrange("p (c s) -> p c s", s=2)[:, :, 1]
            pool.affine_select(out=v0, in_=v0, compare_op=ALU.not_equal, fill=-1.0, base=0,
                               pattern=[[-2, P // 2]], channel_multiplier=1)
            for k in range(1, LEVELS):
                b = 1 << k
                v = join[:, k, :].rearrange("p (c s w) -> p c s w", s=2, w=b)[:, :, 0, :]
                link(pool.memset(v, -1.0))
                link(pool.affine_select(out=v, in_=v, compare_op=ALU.is_ge, fill=0.0, base=-b,
                                        pattern=[[-2 * b, P // (2 * b)], [0, b]], channel_multiplier=1))
                last = pool.affine_select(out=v, in_=v, compare_op=ALU.is_ge, fill=0.0, base=2 * b - 1,
                                          pattern=[[2 * b, P // (2 * b)], [0, b]], channel_multiplier=-1)
            last.then_inc(consts, 1)

            pool.memset(rkT_all[:, :, 0:1], 0.0).then_inc(zero_done, 1)
            for h in range(H):
                pool.memset(S[h][:, :, :], 0.0).then_inc(zero_done, 1)

            pool.nop().then_inc(rkT_kept, H)
            with pool.Fori(0, N) as n:
                for h in range(H):
                    pool.wait_ge(rkT_sb, done(n, h))
                    pool.tensor_copy(rkT_all[:, TILES * h:TILES * h + TILES, bass.ds(n * P + 1, P)],
                                     rkTs[h][:, :, :]).then_inc(rkT_kept, 1)

            pool.wait_ge(scale_ready, 1)
            pool.partition_all_reduce(wmax[:, 4:8], wmax[:, 0:4], P, RMAX).then_inc(scale_ready, 1)
            pool.wait_ge(rkT_kept, H + N * H)

            def keys(n, h):
                a = att[h]
                pool.wait_ge(a["x1"], nth(n))
                pool.tensor_copy(wkx[h][:, :, :],
                                 rkT_all[:, TILES * h:TILES * h + TILES, bass.ds(n * P, P + 1)]).then_inc(a["wkx"], 1)
                for q in range(3):
                    ins = pool.tensor_tensor(ldU[h][:, q, :, :], upto[:, :].unsqueeze(1).to_broadcast([P, TILES, P]),
                                             bc(ldp[:, q, bass.ds(n * B + TILES * h, TILES)], P), ALU.mult)
                ins.then_inc(a["ldU"], 1)

            def first_level(n, h):
                a = att[h]
                pool.wait_ge(a["expB"], nth(n))
                pool.tensor_tensor(rkd[h][:, :, :], wkx[h][:, :, 1:P + 1], expB[h][:, :, :],
                                   ALU.mult).then_inc(a["rkd"], 1)
                pool.wait_ge(a["LT"], nth(n))
                pool.tensor_tensor(Tn[h][:, :, :], LT[h][:, :, :],
                                   join[:, 0, :].unsqueeze(1).to_broadcast([P, TILES, P]), ALU.mult).then_inc(a["tmp0"], 1)
                pool.wait_ge(a["tmp0"], nth(n))
                pool.tensor_tensor(XT[h][:, :, :], Tn[h][:, :, :],
                                   ident[:, :].unsqueeze(1).to_broadcast([P, TILES, P]), ALU.add).then_inc(a["XT0"], 1)

            for h in range(H):
                keys(0, h)
            for h in range(H):
                first_level(0, h)
            with pool.Fori(0, N - 1) as n:
                for h in range(H):
                    keys(n + 1, h)
                    first_level(n + 1, h)

        @block.scalar
        def _(act):
            small = [(wwf[:, :], W_write), (wof[:, :], W_read), (wrf[:, :], Wr), (b2_sb[:, :], b2),
                     (b1r[:, :], b1.rearrange("e (c p) -> (e c) p", p=P)),
                     (wab[:, 0:1], W_alpha.rearrange("h d -> d h")), (wab[:, 1:2], W_beta.rearrange("h d -> d h")),
                     (alog[:, :], row(A_log).to_broadcast([P, 1])), (dtb[:, :], row(dt_bias).to_broadcast([P, 1])),
                     (br_bc[:, :], row(br).to_broadcast([P, E]))]
            assert len(small) == NSMALL
            for dst, src in small:
                act.dma_start(dst, src).then_inc(small_landed, 16)

            act.wait_ge(small_landed, 16 * NSMALL)
            act.activation(nega[:, :], alog[:, :], ACT.Exp).then_inc(act_link, 1)

            act.wait_ge(wT_ps, 2)
            act.activation(WwT[:, :], bank[6][:, 0:P], ACT.Copy).then_inc(wT_sb, 1)
            act.activation(WoT[:, :], bank[6][:, P:2 * P], ACT.Copy).then_inc(wT_sb, 1)

            with act.Fori(0, N) as n:
                for h in range(H):
                    act.wait_ge(rkT_ps, H + done(n, h))
                    act.wait_ge(rkT_kept, done(n, h))
                    act.activation(rkTs[h][:, :, :], tl(h), ACT.Copy).then_inc(rkT_sb, 1)

            act.wait_ge(exp_in, 1)
            act.activation(sc["ua"][:, :], sc["na"][:, :], ACT.Exp).then_inc(act_link, 1)
            act.activation(sc["ub"][:, :], sc["nb"][:, :], ACT.Exp).then_inc(exp_out, 1)
            act.activation(sc["num"][:, :], sc["mb"][:, :], ACT.Exp).then_inc(exp_out, 1)
            act.wait_ge(act_link, 2)
            act.activation(sc["la"][:, :], sc["ua"][:, :], ACT.Ln, bias=1.0).then_inc(exp_out, 1)
            act.wait_ge(cum_ps, 3)
            for k, name in enumerate(("dexp", "ced", "tail")):
                act.activation(sc[name][:, :], bank[0][:, k * G:k * G + G], ACT.Exp).then_inc(exp_out, 1)

            act.wait_ge(cols_ready, 1)

            def scaled(dst, bk, name, n, h):
                for i in range(TILES):
                    ins = act.activation(dst[h][:, i, :], tl(bk)[:, i, :], ACT.Copy, scale=col(sc[name], n, h, i))
                return ins

            def att_keys(n, h, bk):
                act.wait_ge(att[h]["wkT_ps"], nth(n))
                scaled(wkt, bk[0], "tail", n, h).then_inc(att[h]["wkt"], 1)

            def att_expB(n, h, bk):
                act.wait_ge(att[h]["B_ps"], nth(n))
                act.activation(expB[h][:, :, :], tl(bk[0]), ACT.Exp).then_inc(att[h]["expB"], 1)

            def att_dec(n, h, bk):
                act.wait_ge(att[h]["D_ps"], nth(n))
                act.activation(dec[h][:, :, :], tl(bk[0]), ACT.Exp).then_inc(att[h]["dec"], 1)

            def att_v(n, h, bk):
                act.wait_ge(att[h]["V_ps"], nth(n))
                scaled(V, bk[0], "nrm", n, h).then_inc(att[h]["V"], 1)

            def att_x0(n, h, bk):
                act.wait_ge(att[h]["X0_ps"], nth(n))
                act.activation(X[h][:, :, :], tl(bk[2]), ACT.Copy).then_inc(att[h]["X0"], 1)

            def att_xt(n, h, bk, k):
                act.wait_ge(att[h]["turn_ps"], nth(n, LEVELS - 2, k - 1))
                act.activation(XT[h][:, :, :], tl(bk[2]), ACT.Copy).then_inc(att[h]["XT"], 1)

            def att_vnew(n, h, bk):
                act.wait_ge(att[h]["VN_ps"], nth(n))
                scaled(vnew, bk[0], "beta", n, h).then_inc(att[h]["vnew"], 1)

            def att_oT(n, h, bk):
                act.wait_ge(att[h]["OT_ps"], nth(n))
                act.activation(oT[h][:, :, :], tl(bk[2]), ACT.Copy).then_inc(att[h]["oT"], 1)

            def split_high(e):
                act.activation(w1p[:, 0, e, :], w1f[:, e, :], ACT.Copy, scale=wmax[:, 4:5]).then_inc(w_hi, 1)
                act.activation(w2p[:, 0, e, :, :], w2f[:, e, :, :], ACT.Copy, scale=wmax[:, 5:6]).then_inc(w_hi, 1)

            def att_at(u, n, h):
                bk = ATT
                if u == 0:
                    att_keys(n, h, bk)
                if u == 1:
                    att_expB(n, h, bk)
                if u == 3:
                    att_dec(n, h, bk)
                if u == 4:
                    att_v(n, h, bk)
                if u == 7:
                    att_x0(n, h, bk)
                if u in TURN_AT:
                    att_xt(n, h, bk, TURN_AT.index(u) + 1)
                if u == 20:
                    att_vnew(n, h, bk)
                if u == 21:
                    att_oT(n, h, bk)

            def prep_at(u, n, h):
                if u == 5:
                    act.wait_ge(m["xnT_ps"], done(n, h))
                    act.activation(xp[h][:, 0, :, :], tl(PREP), ACT.Copy, scale=X_SCALE).then_inc(m["xhi"], 1)
                if u == 10:
                    act.wait_ge(m["lg"], done(n, h))
                    act.activation(pe_[:, :, :], lg[:, :, :], ACT.Exp).then_inc(m["e"], 1)
                if u == 22:
                    act.wait_ge(m["gT_ps"], done(n, h))
                    act.activation(gT[h][:, :, :], bank[PREP][0:E, :].rearrange("p (t c) -> p t c", t=TILES),
                                   ACT.Copy).then_inc(m["gT"], 1)

            def slot(moe, prep, attn):
                n, h = moe
                for u in range(UNITS):
                    e, c = divmod(u, FB)
                    act.wait_ge(m["up_ps"], done(n, h, UNITS, u))
                    act.wait_ge(m["hlo"], done(n, h, UNITS, u))
                    act.activation(hf[u % 2], bank[UP[u % 2]][:, :], ACT.Relu, bias=b1s[:, e, c:c + 1]).then_inc(m["hf"], 1)
                    if c == 0:
                        act.wait_ge(m["dn_ps"], done(n, h, E, e))
                    act.activation(hp[e % 2][:, 0, c, :], bank[UP[u % 2]][:, :], ACT.Relu,
                                   bias=b1s[:, e, c:c + 1]).then_inc(m["hhi"], 1)
                    if attn:
                        att_at(u, *attn)
                    if prep:
                        prep_at(u, *prep)

            for stage in (att_keys, att_expB, att_dec, att_v, att_x0):
                for h in range(H):
                    stage(0, h, ATT_FIRST[h])
            act.wait_ge(scale_ready, 3)
            for k in range(1, LEVELS - 1):
                if k < 5:
                    split_high(2 * k - 2)
                    split_high(2 * k - 1)
                for h in range(H):
                    att_xt(0, h, ATT_FIRST[h], k)
            for stage in (att_vnew, att_oT):
                for h in range(H):
                    stage(0, h, ATT_FIRST[h])
            for u in range(UNITS):
                prep_at(u, 0, 0)
            act.nop().then_inc(m["hhi"], 2)
            act.wait_ge(w_lo, 2 * E)
            with act.Fori(0, N - 1) as n:
                slot((n, 0), (n, 1), (n + 1, 0))
                slot((n, 1), (n + 1, 0), (n + 1, 1))
            slot((N - 1, 0), (N - 1, 1), None)
            slot((N - 1, 1), None, None)

        @block.vector
        def _(dve):
            count = [0]

            def link(ins):
                count[0] += 1
                ins.then_inc(dve_link, 1)
                dve.wait_ge(dve_link, count[0])

            def rsqrt(x, y, q, link):
                link(dve.tensor_scalar(y.bitcast(I32), x.bitcast(I32), -0.5, RSQRT_SEED, ALU.mult, ALU.add))
                for _ in range(3):
                    link(dve.scalar_tensor_tensor(q, y, -0.5, y, ALU.mult, ALU.mult))
                    link(dve.tensor_tensor(q, q, x, ALU.mult))
                    link(dve.scalar_tensor_tensor(y, q, 1.5, y, ALU.add, ALU.mult))

            for n in range(N):
                dve.wait_ge(x_landed[n], 16)
                for b in range(B):
                    dve.bn_stats(stats[:, n * B + b, :], x_all[:, n, b, :]).then_inc(stats_done, 1)
            dve.wait_ge(stats_done, G)
            for g in range(G):
                last = dve.bn_aggr(mv[:, g, :], stats[:, g, :])
            link(last)
            mean, var = mv[:, :, 0], mv[:, :, 1]
            link(dve.tensor_scalar(sc["ve"][:, :], var, LN_EPS, None, ALU.add))
            rsqrt(sc["ve"][:, :], sc["rstd"][:, :], sc["q"][:, :], link)
            link(dve.tensor_tensor(sc["q"][:, :], sc["rstd"][:, :], sc["rstd"][:, :], ALU.mult))
            link(dve.scalar_tensor_tensor(sc["n2"][:, :], var, float(D), sc["q"][:, :], ALU.mult, ALU.mult))
            link(dve.tensor_scalar(sc["n2"][:, :], sc["n2"][:, :], 1e-24, None, ALU.max))
            rsqrt(sc["n2"][:, :], sc["rn"][:, :], sc["q"][:, :], link)
            dve.tensor_tensor(sc["nrm"][:, :], sc["n2"][:, :], sc["rn"][:, :], ALU.mult)
            dve.tensor_scalar(sc["one"][:, :], sc["rstd"][:, :], 1.0, None, ALU.add)
            dve.tensor_tensor(sc["mr"][:, :], mean, sc["rstd"][:, :], ALU.mult)
            link(dve.tensor_tensor(sc["f"][:, :], sc["rstd"][:, :], sc["rn"][:, :], ALU.mult))

            with dve.Fori(0, N) as n:
                for h in range(H):
                    dve.wait_ge(rkT_ps, done(n, h))
                    for i in range(TILES):
                        ins = dve.tensor_scalar(rk[h][:, i, :], xg(n, h)[:, i, :],
                                                mv[:, bass.ds(n * B + (TILES * h + i), 1), 0], col(sc["f"], n, h, i),
                                                ALU.subtract, ALU.mult)
                    ins.then_inc(rk_made, 1)
                    for i in range(TILES):
                        dve.tensor_scalar(xg(n, h)[:, i, :], xg(n, h)[:, i, :], col(sc["one"], n, h, i),
                                          col(sc["mr"], n, h, i), ALU.mult, ALU.subtract).then_inc(base_ready, 1)
                    dve.wait_ge(z_ps, done(n, h))
                    dve.tensor_copy(z_all[:, bass.ds(n * B + TILES * h, TILES), :],
                                    bank[2 + h][:, 0:2 * TILES].rearrange("p (t c) -> p t c", c=2)).then_inc(z_sb, 1)

            s = {k: t[:, :] for k, t in sc.items()}
            dve.wait_ge(z_sb, N * H)
            dve.wait_ge(small_landed, 16 * NSMALL)
            link(dve.tensor_tensor(s["za"], z_all[:, :, 0], s["nrm"], ALU.mult))
            link(dve.tensor_tensor(s["zb"], z_all[:, :, 1], s["nrm"], ALU.mult))
            link(dve.tensor_scalar(s["za"], s["za"], dtb[:, :], None, ALU.add))
            link(dve.scalar_tensor_tensor(s["na"], s["za"], -1.0, s["za"], ALU.mult, ALU.min))
            link(dve.scalar_tensor_tensor(s["nb"], s["zb"], -1.0, s["zb"], ALU.mult, ALU.min))
            dve.tensor_scalar(s["mb"], s["zb"], 0.0, None, ALU.min).then_inc(exp_in, 1)
            dve.wait_ge(exp_out, 3)
            link(dve.scalar_tensor_tensor(s["la"], s["za"], 0.0, s["la"], ALU.max, ALU.add))
            dve.wait_ge(act_link, 1)
            link(dve.tensor_scalar(nega[:, :], nega[:, :], -1.0, None, ALU.mult))
            dve.tensor_scalar(s["ld"], s["la"], nega[:, :], None, ALU.mult).then_inc(ld_ready, 1)
            dve.wait_ge(ld_ready, 1)
            link(dve.tensor_copy(ldp[:, 0, :], s["ld"]))
            link(dve.tensor_tensor(s["ldr"], s["ld"], ldp[:, 0, :], ALU.subtract))
            link(dve.tensor_copy(ldp[:, 1, :], s["ldr"]))
            dve.tensor_tensor(ldp[:, 2, :], s["ldr"], ldp[:, 1, :], ALU.subtract).then_inc(ld_ready, 1)
            link(dve.tensor_scalar(s["den"], s["ub"], 1.0, None, ALU.add))
            link(dve.reciprocal(s["den"], s["den"]))
            link(dve.tensor_tensor(s["beta"], s["den"], s["num"], ALU.mult))
            dve.wait_ge(exp_out, 6)
            dve.tensor_scalar(s["ndexp"], s["dexp"], -1.0, None, ALU.mult).then_inc(cols_ready, 1)

            dve.wait_ge(w1_landed, 16)
            dve.wait_ge(w2_landed, 16 * E)
            dve.wait_ge(b1T_ps, 1)
            for k, t in enumerate((w1f[:, :, :].rearrange("p e f -> p (e f)"),
                                   w2f[:, :, :, :].rearrange("p e c d -> p (e c d)"), wrf[:, :],
                                   bank[7][:, 0:E * FB])):
                last = dve.tensor_reduce(wmax[:, k:k + 1], t, AX_X, ALU.max, apply_absolute_value=True)
            last.then_inc(scale_ready, 1)

            dve.wait_ge(scale_ready, 2)
            link(dve.scalar_tensor_tensor(wmax[:, 4:5], wmax[:, 4:5], float(P), wmax[:, 7:8], ALU.mult, ALU.add))
            link(dve.tensor_scalar(wmax[:, 4:7], wmax[:, 4:7], 1e-30, None, ALU.max))
            link(dve.tensor_scalar(wmax[:, 4:7].bitcast(I32), wmax[:, 4:7].bitcast(I32), 0x7F800000, None, ALU.bitwise_and))
            link(dve.reciprocal(wmax[:, 4:7], wmax[:, 4:7]))
            link(dve.tensor_scalar(wmax[:, 4:5], wmax[:, 4:5], 2.0 ** 14 / X_SCALE, None, ALU.mult))
            link(dve.tensor_scalar(wmax[:, 5:7], wmax[:, 5:7], 2.0 ** 12, None, ALU.mult))
            link(dve.tensor_scalar(wmax[:, 0:1], wmax[:, 6:7], X_SCALE, None, ALU.mult))
            link(dve.scalar_tensor_tensor(wmax[:, 1:2], wmax[:, 4:5], X_SCALE, wmax[:, 5:6], ALU.mult, ALU.mult))
            link(dve.reciprocal(wmax[:, 0:2], wmax[:, 0:2]))
            link(dve.tensor_scalar(b1s[:, :, :].rearrange("p e c -> p (e c)"), bank[7][:, 0:E * FB], wmax[:, 4:5], X_SCALE,
                                   ALU.mult, ALU.mult))
            link(dve.tensor_scalar(wrp[:, 0, :], wrf[:, :], wmax[:, 6:7], None, ALU.mult))
            link(dve.scalar_tensor_tensor(wrp[:, 1, :], wrf[:, :], wmax[:, 6:7], wrp[:, 0, :], ALU.mult, ALU.subtract))
            dve.nop().then_inc(scale_ready, 1)

            dve.wait_ge(zero_done, 1 + H)
            dve.wait_ge(base_ready, G)
            for h in range(H):
                dve.nop().then_inc(att[h]["S"], 1)
                dve.nop().then_inc(att[h]["x1"], 1)

            def att_products(n, h, bk):
                a = att[h]
                dve.wait_ge(a["gq_ps"], nth(n))
                dve.wait_ge(a["dec"], nth(n))
                for i in range(TILES):
                    ins = dve.scalar_tensor_tensor(LT[h][:, i, :], gq(bk)[i // 2][:, i % 2, 0:P], col(sc["beta"], n, h, i),
                                                   dec[h][:, i, :], ALU.mult, ALU.mult)
                ins.then_inc(a["LT"], 1)
                for c in range(2):
                    ins = dve.tensor_tensor(intraT[h][:, 2 * c:2 * c + 2, :], gq(bk)[c][:, :, 1:P + 1],
                                            dec[h][:, 2 * c:2 * c + 2, :], ALU.mult)
                ins.then_inc(a["intra"], 1)

            def att_r(n, h, bk):
                a = att[h]
                dve.wait_ge(a["WS_ps"], nth(n))
                dve.wait_ge(a["V"], nth(n))
                for i in range(TILES):
                    ins = dve.scalar_tensor_tensor(R[h][:, i, :], tl(bk[1])[:, i, :], col(sc["ndexp"], n, h, i),
                                                   V[h][:, i, :], ALU.mult, ALU.add)
                ins.then_inc(a["R"], 1)

            def att_tn(n, h, bk, k):
                a = att[h]
                dve.wait_ge(a["T_ps"], nth(n, LEVELS - 1, k - 1))
                dve.tensor_tensor(Tn[h][:, :, :], tl(bk[0]), join[:, k, :].unsqueeze(1).to_broadcast([P, TILES, P]),
                                  ALU.mult).then_inc(a["Tn"], 1)

            def att_x(n, h, bk, k):
                a = att[h]
                if k < LEVELS - 1:
                    dve.wait_ge(a["XC_ps"], nth(n, LEVELS - 2, k - 1))
                    dve.tensor_tensor(X[h][:, :, :], tl(bk[1]), X[h][:, :, :], ALU.add).then_inc(a["X"], 1)
                else:
                    dve.wait_ge(a["last_ps"], nth(n))
                    dve.tensor_tensor(XT[h][:, :, :], tl(bk[1]), XT[h][:, :, :], ALU.add).then_inc(a["A"], 1)

            def att_s(n, h, bk):
                a = att[h]
                dve.wait_ge(a["SN_ps"], nth(n))
                dve.wait_ge(a["OT_ps"], nth(n))
                for i in range(TILES):
                    ins = dve.scalar_tensor_tensor(S[h][:, i, :], S[h][:, i, :], col(sc["ced"], n, h, i),
                                                   tl(bk[1])[:, i, :], ALU.mult, ALU.add)
                ins.then_inc(a["S"], 1)

            def att_x1(n, h, bk):
                dve.wait_ge(att[h]["O_ps"], nth(n))
                dve.tensor_tensor(xg(n, h), tl(bk[0]), xg(n, h), ALU.add).then_inc(att[h]["x1"], 1)

            def split_low(e):
                for k, (wf, wp) in enumerate(((w1f[:, e, :], w1p[:, :, e, :]),
                                              (w2words[:, e * F:e * F + F], w2p[:, :, e, :, :].rearrange("p a c d -> p a (c d)")))):
                    dve.wait_ge(w_hi, 2 * e + k + 1)
                    dve.scalar_tensor_tensor(wp[:, 1, :], wf, wmax[:, 4 + k:5 + k], wp[:, 0, :], ALU.mult,
                                             ALU.subtract).then_inc(w_lo, 1)

            def att_at(u, n, h):
                bk = ATT
                if u == 4:
                    att_products(n, h, bk)
                if u == 6:
                    att_r(n, h, bk)
                if u in T_AT:
                    att_tn(n, h, bk, T_AT.index(u) + 1)
                if u - 1 in T_AT:
                    att_x(n, h, bk, T_AT.index(u - 1) + 1)
                if u == 22:
                    att_s(n, h, bk)
                if u == 23:
                    att_x1(n, h, bk)

            LINKS = 40
            r = {k: t[:, :] for k, t in mr_.items()}
            pj = pr[:, :, :].unsqueeze(2).to_broadcast([P, TILES, E, E])
            pe = pr[:, :, :].unsqueeze(3).to_broadcast([P, TILES, E, E])
            tri = ge_tri[:, :, :].unsqueeze(1).to_broadcast([P, TILES, E, E])
            cnt = [0]

            def prep_at(u, n, h):
                if u == 0:
                    cnt[0] = 0

                def mlink(ins):
                    cnt[0] += 1
                    ins.then_inc(m["link"], 1)

                def prior():
                    dve.wait_ge(m["link"], n * (H * LINKS) + (h * LINKS + cnt[0]))

                if u == 0:
                    dve.wait_ge(att[h]["x1"], 1 + nth(n))
                    dve.sem_inc(m["link"], 1)
                    cnt[0] += 1
                    for i in range(TILES):
                        last = dve.bn_stats(mst[:, i, :], xg(n, h)[:, i, :])
                    mlink(last)
                if u == 1:
                    prior()
                    dve.sem_inc(m["link"], 1)
                    cnt[0] += 1
                    for i in range(TILES):
                        last = dve.bn_aggr(mmv[:, i, :], mst[:, i, :])
                    mlink(last)
                    prior()
                    mlink(dve.tensor_scalar(r["ve"], mmv[:, :, 1], LN_EPS, None, ALU.add))
                if u == 2:
                    prior()
                    mlink(dve.tensor_scalar(r["r"].bitcast(I32), r["ve"].bitcast(I32), -0.5, RSQRT_SEED, ALU.mult, ALU.add))
                if u in (2, 3, 4):
                    prior()
                    mlink(dve.scalar_tensor_tensor(r["q"], r["r"], -0.5, r["r"], ALU.mult, ALU.mult))
                    prior()
                    mlink(dve.tensor_tensor(r["q"], r["q"], r["ve"], ALU.mult))
                    prior()
                    mlink(dve.scalar_tensor_tensor(r["r"], r["q"], 1.5, r["r"], ALU.add, ALU.mult))
                if u == 4:
                    prior()
                    for i in range(TILES):
                        last = dve.tensor_scalar(xn[h][:, i, :], xg(n, h)[:, i, :], mmv[:, i, 0:1], mr_["r"][:, i:i + 1],
                                                 ALU.subtract, ALU.mult)
                    last.then_inc(m["xn"], 1)
                if u == 6:
                    dve.wait_ge(m["xhi"], done(n, h))
                    dve.scalar_tensor_tensor(xp[h][:, 1, :, :], tl(PREP), X_SCALE, xp[h][:, 0, :, :], ALU.mult,
                                             ALU.subtract).then_inc(m["xlo"], 1)
                if u == 8:
                    dve.wait_ge(m["lg_ps"], done(n, h))
                    mlink(dve.scalar_tensor_tensor(lg[:, :, :], bank[PREP][:, 0:TILES * E].rearrange("p (t e) -> p t e", e=E),
                                                   wmax[:, 0:1], br_bc[:, :].unsqueeze(1).to_broadcast([P, TILES, E]),
                                                   ALU.mult, ALU.add))
                    prior()
                    mlink(dve.tensor_reduce(r["mx"], lg[:, :, :], AX_X, ALU.max))
                if u == 9:
                    prior()
                    dve.tensor_tensor(lg[:, :, :], lg[:, :, :], bc(r["mx"], E), ALU.subtract).then_inc(m["lg"], 1)
                if u == 11:
                    dve.wait_ge(m["e"], done(n, h))
                    mlink(dve.tensor_reduce(r["sum"], pe_[:, :, :], AX_X, ALU.add))
                    prior()
                    mlink(dve.reciprocal(r["rs"], r["sum"]))
                if u == 12:
                    prior()
                    mlink(dve.tensor_tensor(pr[:, :, :], pe_[:, :, :], bc(r["rs"], E), ALU.mult))
                if u == 13:
                    prior()
                    mlink(dve.tensor_tensor(cmp1[:, :, :, :], pj, pe, ALU.is_ge))
                    mlink(dve.tensor_tensor(cmp2[:, :, :, :], pj, pe, ALU.is_gt))
                if u == 14:
                    prior()
                    mlink(dve.tensor_tensor(cmp1[:, :, :, :], cmp1[:, :, :, :], tri, ALU.mult))
                if u == 15:
                    prior()
                    mlink(dve.tensor_tensor(cmp1[:, :, :, :], cmp1[:, :, :, :], cmp2[:, :, :, :], ALU.max))
                if u == 16:
                    prior()
                    mlink(dve.tensor_tensor(cmp1[:, :, :, :], cmp1[:, :, :, :], pj, ALU.mult))
                if u == 17:
                    prior()
                    mlink(dve.tensor_reduce(cumt[:, :, :], cmp1[:, :, :, :], AX_X, ALU.add))
                if u == 18:
                    prior()
                    mlink(dve.tensor_scalar(k1[:, :, :], cumt[:, :, :], TOP_P, None, ALU.is_lt))
                    mlink(dve.tensor_tensor(k2[:, :, :], cumt[:, :, :], pr[:, :, :], ALU.is_le))
                if u == 19:
                    prior()
                    mlink(dve.tensor_tensor(k1[:, :, :], k1[:, :, :], k2[:, :, :], ALU.max))
                if u == 20:
                    prior()
                    dve.tensor_tensor(gate[h][:, :, :], pr[:, :, :], k1[:, :, :], ALU.mult).then_inc(m["gate"], 1)
                if u == 21:
                    dve.wait_ge(m["gate"], done(n, h))
                    mlink(dve.tensor_scalar(gates[h][:, :, :], gate[h][:, :, :], wmax[:, 1:2], None, ALU.mult))
                if u == 26:
                    prior()
                    dve.wait_ge(m["b2_ps"], done(n, h))
                    dve.tensor_tensor(xg(n, h), tl(PREP), xg(n, h), ALU.add).then_inc(m["acc0"], 1)
                    assert cnt[0] <= LINKS
                    if cnt[0] < LINKS:
                        dve.nop().then_inc(m["link"], LINKS - cnt[0])

            def slot(moe, prep, attn):
                n, h = moe

                def gather(e, i):
                    if i == 0:
                        dve.wait_ge(m["dn_ps"], 2 + done(n, h, E, e))
                        if e == 0:
                            dve.wait_ge(m["acc0"], done(n, h))
                        else:
                            dve.wait_ge(m["acc"], 2 + done(n, h, E, e - 1))
                    ins = dve.scalar_tensor_tensor(xg(n, h)[:, i, :], tl(DOWN[e % 2])[:, i, :], gates[h][:, i, e:e + 1],
                                                   xg(n, h)[:, i, :], ALU.mult, ALU.add)
                    if i == TILES - 1:
                        ins.then_inc(m["acc"], 1)

                for u in range(UNITS):
                    e, c = divmod(u, FB)
                    if attn:
                        att_at(u, *attn)
                    dve.wait_ge(m["hf"], done(n, h, UNITS, u))
                    dve.wait_ge(m["hhi"], 2 + done(n, h, UNITS, u))
                    dve.tensor_tensor(hp[e % 2][:, 1, c, :], hf[u % 2], hp[e % 2][:, 0, c, :],
                                      ALU.subtract).then_inc(m["hlo"], 1)
                    if e >= 2:
                        gather(e - 2, c)
                    if prep:
                        prep_at(u, *prep)
                for e in (E - 2, E - 1):
                    for i in range(TILES):
                        gather(e, i)

            for stage in (att_products, att_r):
                for h in range(H):
                    stage(0, h, ATT_FIRST[h])
            for k in range(1, LEVELS):
                for h in range(H):
                    att_tn(0, h, ATT_FIRST[h], k)
                for h in range(H):
                    att_x(0, h, ATT_FIRST[h], k)
                if k < 5:
                    split_low(2 * k - 2)
                    split_low(2 * k - 1)
            for stage in (att_s, att_x1):
                for h in range(H):
                    stage(0, h, ATT_FIRST[h])
            for u in range(UNITS):
                prep_at(u, 0, 0)
            dve.nop().then_inc(m["hlo"], 2)
            dve.nop().then_inc(m["acc"], 2)
            with dve.Fori(0, N - 1) as n:
                slot((n, 0), (n, 1), (n + 1, 0))
                slot((n, 1), (n + 1, 0), (n + 1, 1))
            slot((N - 1, 0), (N - 1, 1), None)
            slot((N - 1, 1), None, None)

        @block.tensor
        def _(pe):
            pe.wait_ge(consts, 1)
            pe.wait_ge(small_landed, 16 * NSMALL)
            pe.transpose(bank[6][:, 0:P], wwf[:, :], ident[:, :]).then_inc(wT_ps, 1)
            pe.transpose(bank[6][:, P:2 * P], wof[:, :], ident[:, :]).then_inc(wT_ps, 1)
            pe.transpose(bank[7][:, 0:E * FB], b1r[:, :], ident[0:E * FB, 0:E * FB]).then_inc(b1T_ps, 1)

            pe.nop().then_inc(rkT_ps, H)
            with pe.Fori(0, N) as n:
                for h in range(H):
                    pe.wait_ge(rk_made, done(n, h))
                    for i in range(TILES):
                        ins = pe.transpose(tl(h)[:, i, :], rk[h][:, i, :], ident[:, :])
                    ins.then_inc(rkT_ps, 1)
                    pe.wait_ge(rkT_sb, done(n, h))
                    for i in range(TILES):
                        ins = pe.matmul(bank[2 + h][:, 2 * i:2 * i + 2], rkTs[h][:, i, :], wab[:, :], start=True, stop=True)
                    ins.then_inc(z_ps, 1)

            pe.wait_ge(ld_ready, 1)
            pe.matmul(bank[0][:, 0:G], upto[:, :], sc["ld"][:, :], start=True, stop=True).then_inc(cum_ps, 1)
            pe.matmul(bank[0][:, G:2 * G], ones[:, :], sc["ld"][:, :], start=True, stop=True).then_inc(cum_ps, 1)
            pe.matmul(bank[0][:, 2 * G:3 * G], after[:, :], sc["ld"][:, :], start=True, stop=True).then_inc(cum_ps, 1)

            pe.wait_ge(wT_sb, 2)
            pe.wait_ge(cols_ready, 1)

            def att_keys(n, h, bk):
                a = att[h]
                pe.wait_ge(a["x1"], nth(n))
                pe.wait_ge(a["wkx"], nth(n))
                for i in range(TILES):
                    ins = pe.transpose(tl(bk[0])[:, i, :], wkx[h][:, i, 0:P], ident[:, :])
                ins.then_inc(a["wkT_ps"], 1)

            def att_b(n, h, bk):
                a = att[h]
                pe.wait_ge(a["ldU"], nth(n))
                pe.wait_ge(a["wkt"], nth(n))
                for q in range(3):
                    ins = pe.matmul(bank[bk[0]][:, :], ones_b[:, :], ldU[h][:, q, :, :].rearrange("p t c -> p (t c)"),
                                    start=(q == 0), stop=(q == 2))
                ins.then_inc(a["B_ps"], 1)

            def att_gq(n, h, bk):
                for i in range(TILES):
                    ins = pe.matmul(gq(bk)[i // 2][:, i % 2, :], wkx[h][:, i, 0:P], wkx[h][:, i, :], start=True, stop=True)
                ins.then_inc(att[h]["gq_ps"], 1)

            def att_d(n, h, bk):
                a = att[h]
                pe.wait_ge(a["expB"], nth(n))
                for q in range(3):
                    pe.matmul(bank[bk[0]][:, :], after_b[:, :], ldU[h][:, q, :, :].rearrange("p t c -> p (t c)"),
                              start=(q == 0), stop=False)
                pe.matmul(bank[bk[0]][:, :], ident_b[:, :], far_b[:, :].unsqueeze(1).to_broadcast([P, TILES, P]),
                          start=False, stop=True).then_inc(a["D_ps"], 1)

            def att_v(n, h, bk):
                a = att[h]
                pe.wait_ge(a["dec"], nth(n))
                for i in range(TILES):
                    ins = pe.matmul(tl(bk[0])[:, i, :], wkx[h][:, i, 1:P + 1], WwT[:, :], start=True, stop=True)
                ins.then_inc(a["V_ps"], 1)

            def att_ws(n, h, bk):
                a = att[h]
                pe.wait_ge(a["intra"], nth(n))
                pe.wait_ge(a["S"], nth(n))
                for i in range(TILES):
                    ins = pe.matmul(tl(bk[1])[:, i, :], wkx[h][:, i, 0:P], S[h][:, i, :], start=True, stop=True)
                ins.then_inc(a["WS_ps"], 1)

            def att_x0(n, h, bk):
                a = att[h]
                pe.wait_ge(a["XT0"], nth(n))
                for i in range(TILES):
                    ins = pe.transpose(tl(bk[2])[:, i, :], XT[h][:, i, :], ident[:, :])
                ins.then_inc(a["X0_ps"], 1)

            def att_t(n, h, bk, k):
                a = att[h]
                if k == 1:
                    pe.wait_ge(a["X0"], nth(n))
                    pe.wait_ge(a["V"], nth(n))
                else:
                    pe.wait_ge(a["X"], nth(n, LEVELS - 2, k - 2))
                for i in range(TILES):
                    ins = pe.matmul(tl(bk[0])[:, i, :], LT[h][:, i, :], X[h][:, i, :], start=True, stop=True)
                ins.then_inc(a["T_ps"], 1)

            def att_turn(n, h, bk, k):
                for i in range(TILES):
                    ins = pe.transpose(tl(bk[2])[:, i, :], X[h][:, i, :], ident[:, :])
                ins.then_inc(att[h]["turn_ps"], 1)

            def att_xc(n, h, bk, k):
                a = att[h]
                pe.wait_ge(a["Tn"], nth(n, LEVELS - 1, k - 1))
                if k == 1:
                    pe.wait_ge(a["R"], nth(n))
                else:
                    pe.wait_ge(a["XT"], nth(n, LEVELS - 2, k - 2))
                for i in range(TILES):
                    if k < LEVELS - 1:
                        ins = pe.matmul(tl(bk[1])[:, i, :], XT[h][:, i, :], Tn[h][:, i, :], start=True, stop=True)
                    else:
                        ins = pe.matmul(tl(bk[1])[:, i, :], Tn[h][:, i, :], XT[h][:, i, :], start=True, stop=True)
                ins.then_inc(a["XC_ps"] if k < LEVELS - 1 else a["last_ps"], 1)

            def att_vn(n, h, bk):
                a = att[h]
                pe.wait_ge(a["A"], nth(n))
                for i in range(TILES):
                    ins = pe.matmul(tl(bk[0])[:, i, :], XT[h][:, i, :], R[h][:, i, :], start=True, stop=True)
                ins.then_inc(a["VN_ps"], 1)

            def att_so(n, h, bk):
                a = att[h]
                pe.wait_ge(a["vnew"], nth(n))
                pe.wait_ge(a["rkd"], nth(n))
                for i in range(TILES):
                    ins = pe.matmul(tl(bk[1])[:, i, :], wkt[h][:, i, :], vnew[h][:, i, :], start=True, stop=True)
                ins.then_inc(a["SN_ps"], 1)
                for i in range(TILES):
                    pe.matmul(tl(bk[2])[:, i, :], S[h][:, i, :], rkd[h][:, i, :], start=True, stop=False)
                    ins = pe.matmul(tl(bk[2])[:, i, :], vnew[h][:, i, :], intraT[h][:, i, :], start=False, stop=True)
                ins.then_inc(a["OT_ps"], 1)

            def att_o(n, h, bk):
                a = att[h]
                pe.wait_ge(a["oT"], nth(n))
                for i in range(TILES):
                    ins = pe.matmul(tl(bk[0])[:, i, :], oT[h][:, i, :], WoT[:, :], start=True, stop=True)
                ins.then_inc(a["O_ps"], 1)

            def att_at(u, n, h):
                bk = ATT
                for at, stage in ((0, att_keys), (1, att_b), (2, att_gq), (3, att_d), (4, att_v), (5, att_ws), (7, att_x0),
                                  (20, att_vn), (21, att_so), (23, att_o)):
                    if u == at:
                        stage(n, h, bk)
                if u in T_AT:
                    att_t(n, h, bk, T_AT.index(u) + 1)
                if u in TURN_AT:
                    att_turn(n, h, bk, TURN_AT.index(u) + 1)
                if u - 1 in T_AT:
                    att_xc(n, h, bk, T_AT.index(u - 1) + 1)

            def prep_at(u, n, h):
                if u == 5:
                    pe.wait_ge(m["xn"], done(n, h))
                    for i in range(TILES):
                        ins = pe.transpose(tl(PREP)[:, i, :], xn[h][:, i, :], ident[:, :])
                    ins.then_inc(m["xnT_ps"], 1)
                if u == 7:
                    pe.wait_ge(m["xlo"], done(n, h))
                    for i in range(TILES):
                        for a in range(2):
                            for w in range(2):
                                ins = pe.matmul(bank[PREP][:, E * i:E * i + E], xp[h][:, a, i, :], wrp[:, w, :],
                                                start=(a == 0 and w == 0), stop=(a == 1 and w == 1))
                    ins.then_inc(m["lg_ps"], 1)
                if u == 22:
                    pe.wait_ge(m["gate"], done(n, h))
                    for i in range(TILES):
                        ins = pe.transpose(bank[PREP][0:E, i * P:(i + 1) * P], gate[h][:, i, :], ident[:, :])
                    ins.then_inc(m["gT_ps"], 1)
                if u == 24:
                    pe.wait_ge(m["gT"], done(n, h))
                    for i in range(TILES):
                        ins = pe.matmul(tl(PREP)[:, i, :], gT[h][:, i, :], b2_sb[:, :], start=True, stop=True)
                    ins.then_inc(m["b2_ps"], 1)

            def slot(moe, prep, attn):
                n, h = moe

                def up(u):
                    e, c = divmod(u, FB)
                    pe.wait_ge(m["hhi"], done(n, h, UNITS, u))
                    for j, (a, w) in enumerate(((0, 0), (1, 0), (0, 1))):
                        ins = pe.matmul(bank[UP[u % 2]][:, :], w1p[:, w, e, c * P:(c + 1) * P],
                                        xp[h][:, a, :, :].rearrange("p t c -> p (t c)"), start=(j == 0), stop=(j == 2))
                    ins.then_inc(m["up_ps"], 1)

                def down(e, i):
                    if i == 0:
                        pe.wait_ge(m["hlo"], 2 + done(n, h, UNITS, e * FB + FB - 1))
                        pe.wait_ge(m["acc"], done(n, h, E, e))
                    for c in range(FB):
                        for j, (a, w) in enumerate(((0, 0), (0, 1), (1, 0))):
                            ins = pe.matmul(tl(DOWN[e % 2])[:, i, :], hp[e % 2][:, a, c, i * P:(i + 1) * P],
                                            w2p[:, w, e, c, :], start=(c == 0 and j == 0),
                                            stop=(c == FB - 1 and j == 2))
                    if i == TILES - 1:
                        ins.then_inc(m["dn_ps"], 1)

                for u in range(UNITS):
                    e, c = divmod(u, FB)
                    up(u)
                    if attn:
                        att_at(u, *attn)
                    if prep:
                        prep_at(u, *prep)
                    if e >= 1:
                        down(e - 1, c)
                for i in range(TILES):
                    down(E - 1, i)

            for stage in (att_keys, att_b, att_gq, att_d, att_v, att_ws, att_x0):
                for h in range(H):
                    stage(0, h, ATT_FIRST[h])
            for k in range(1, LEVELS):
                for h in range(H):
                    att_t(0, h, ATT_FIRST[h], k)
                    if k > 1:
                        att_turn(0, h, ATT_FIRST[h], k - 1)
                for h in range(H):
                    att_xc(0, h, ATT_FIRST[h], k)
            for stage in (att_vn, att_so, att_o):
                for h in range(H):
                    stage(0, h, ATT_FIRST[h])
            for u in range(UNITS):
                prep_at(u, 0, 0)
            for h in range(H):
                pe.wait_ge(att[h]["x1"], 1 + nth(0))
            pe.wait_ge(w_lo, 2 * E)
            pe.nop().then_inc(m["dn_ps"], 2)
            with pe.Fori(0, N - 1) as n:
                slot((n, 0), (n, 1), (n + 1, 0))
                slot((n, 1), (n + 1, 0), (n + 1, 1))
            slot((N - 1, 0), (N - 1, 1), None)
            slot((N - 1, 1), None, None)


_INS = ['L0_attn_out', 'L0_attn_W_write', 'L0_attn_W_read', 'L0_attn_W_alpha', 'L0_attn_W_beta', 'L0_attn_A_log',
        'L0_attn_dt_bias', 'L0_ffn_Wr', 'L0_ffn_br', 'L0_ffn_W1', 'L0_ffn_b1', 'L0_ffn_W2', 'L0_ffn_b2']


def kernel(**inputs):
    import numpy as _np
    import concourse.bacc as _bacc
    from concourse import mybir as _mybir
    from concourse.bass_utils import run_bass_kernel_spmd as _run

    nc = _bacc.Bacc("TRN2", target_bir_lowering=False, num_devices=1)
    arrays, args = {}, []
    for name in _INS:
        a = _np.ascontiguousarray(inputs[name])
        arrays[f"in_{name}_dram"] = a
        args.append(nc.dram_tensor(f"in_{name}_dram", a.shape, _mybir.dt.from_np(a.dtype), kind="ExternalInput").ap())
    x = inputs['L0_attn_out']
    args.append(nc.dram_tensor("out_0_dram", x.shape, _mybir.dt.float32, kind="ExternalOutput").ap())
    preln_layer(nc, *args)
    r = _run(nc, [arrays], core_ids=[0])
    return r.results[0]["out_0_dram"]
```

```python
from contextlib import ExitStack

import concourse.bass as bass
from concourse import mybir

P = 128
TILES = 4
LEVELS = 7
LN_EPS = 1e-5
TOP_P = 0.8
X_SCALE = 16.0
H_SCALE = 2.0 ** -6
FAR = 1e30
RSQRT_SEED = float(0x5F3759DF)

ALU = mybir.AluOpType
ACT = mybir.ActivationFunctionType
AX_X = mybir.AxisListType.X
F32 = mybir.dt.float32
F16 = mybir.dt.float16
BF16 = mybir.dt.bfloat16
I32 = mybir.dt.int32
RMAX = bass.bass_isa.ReduceOp.max


def preln_layer(nc, x_in, W_write, W_read, W_alpha, W_beta, A_log, dt_bias, Wr, br, W1, b1, W2, b2, out):
    B, T, D = x_in.shape
    E, _, F = W1.shape
    N = T // P
    H = B // TILES
    G = N * B
    FB = F // P
    assert D == P and TILES * P == 512 and B == H * TILES and H == 2 and E == 8

    x_v = x_in.rearrange("b (n p) d -> n p b d", p=P)
    out_v = out.rearrange("b (n p) d -> p n b d", p=P)
    row = lambda v: v.rearrange("(a n) -> a n", a=1)

    ctx = ExitStack()
    with ctx:
        def sb(name, shape, dt=F32):
            return ctx.enter_context(nc.sbuf_tensor(name, shape, dt))

        def sem(name):
            return ctx.enter_context(nc.semaphore(name))

        x_all = sb("x_all", [P, N, B, D])
        rkT_all = sb("rkT_all", [P, B, 1 + T])
        w1f = sb("w1f", [P, E, F])
        w2f = sb("w2f", [P, E, FB, D])
        w1p = sb("w1p", [P, 2, E, F], F16)
        w2p = sb("w2p", [P, 2, E, FB, D], F16)
        wrf = sb("wrf", [P, E])
        wrp = sb("wrp", [P, 2, E], F16)
        wwf = sb("wwf", [P, D])
        wof = sb("wof", [P, D])
        WwT = sb("WwT", [P, D])
        WoT = sb("WoT", [P, D])
        wab = sb("wab", [P, 2])
        alog = sb("alog", [P, 1])
        dtb = sb("dtb", [P, 1])
        nega = sb("nega", [P, 1])
        br_bc = sb("br_bc", [P, E])
        b2_sb = sb("b2_sb", [E, D])
        b1r = sb("b1r", [E * FB, P])
        b1s = sb("b1s", [P, E, FB])

        ident = sb("ident", [P, P])
        ident_b = sb("ident_b", [P, P], BF16)
        ones = sb("ones", [P, P])
        ones_b = sb("ones_b", [P, P], BF16)
        after = sb("after", [P, P])
        after_b = sb("after_b", [P, P], BF16)
        upto = sb("upto", [P, P])
        far_b = sb("far_b", [P, P], BF16)
        join = sb("join", [P, LEVELS, P])
        ge_tri = sb("ge_tri", [P, E, E])

        stats = sb("stats", [P, G, 6])
        mv = sb("mv", [P, G, 2])
        sc = {k: sb("sc_" + k, [P, G]) for k in
              ("nrm", "f", "one", "nmr", "la", "den", "mb", "num", "ld", "ldr", "dexp", "ndexp", "ced", "tail", "beta")}
        s2 = {k: sb("s2_" + k, [P, 2, G]) for k in ("v", "r", "q", "z", "n", "u")}
        ldp = sb("ldp", [P, 3, G], BF16)
        wmax = sb("wmax", [P, 8])
        wsq = sb("wsq", [P, 4])

        rk = [sb(f"rk{h}", [P, TILES, D]) for h in range(H)]
        wkx = [sb(f"wkx{h}", [P, TILES, P + 1]) for h in range(H)]
        ldU = [sb(f"ldU{h}", [P, 3, TILES, P], BF16) for h in range(H)]
        wkt = [sb(f"wkt{h}", [P, TILES, D]) for h in range(H)]
        expB = [sb(f"expB{h}", [P, TILES, P]) for h in range(H)]
        dec = [sb(f"dec{h}", [P, TILES, P]) for h in range(H)]
        rkd = [sb(f"rkd{h}", [P, TILES, P]) for h in range(H)]
        V = [sb(f"V{h}", [P, TILES, D]) for h in range(H)]
        LT = [sb(f"LT{h}", [P, TILES, P]) for h in range(H)]
        intraT = [sb(f"intraT{h}", [P, TILES, P]) for h in range(H)]
        X = [sb(f"X{h}", [P, TILES, P]) for h in range(H)]
        XT = [sb(f"XT{h}", [P, TILES, P]) for h in range(H)]
        Tn = [sb(f"Tn{h}", [P, TILES, P]) for h in range(H)]
        R = [sb(f"R{h}", [P, TILES, D]) for h in range(H)]
        vnew = [sb(f"vnew{h}", [P, TILES, D]) for h in range(H)]
        oT = [sb(f"oT{h}", [P, TILES, P]) for h in range(H)]
        S = [sb(f"S{h}", [P, TILES, D]) for h in range(H)]

        xn = rk
        xp = [sb(f"xp{h}", [P, 2, TILES, P], F16) for h in range(H)]
        w2words = w2f[:, :, :, :].rearrange("p e c d -> p (e c d)")
        squares = (w2p[:, :, :, :, :].rearrange("p a e c d -> p (a e c d)").bitcast(F32),
                   w1p[:, :, :, :].rearrange("p a e f -> p (a e f)").bitcast(F32))
        hf = [w2words[:, 512 * i:512 * (i + 1)] for i in range(2)]
        hp = [w1f[:, E // 2 * i:E // 2 * (i + 1), :].rearrange("p e f -> p (e f)").bitcast(F16).rearrange(
            "p (a c t) -> p a c t", a=2, c=FB) for i in range(2)]
        mst = sb("mst", [P, TILES, 6])
        mmv = sb("mmv", [P, TILES, 2])
        mr_ = {k: sb("m_" + k, [P, TILES]) for k in ("ve", "r", "q", "mx", "sum", "rs")}
        lg = sb("lg", [P, TILES, E])
        pe_ = sb("pe_", [P, TILES, E])
        pr = sb("pr", [P, TILES, E])
        cmp1 = sb("cmp1", [P, TILES, E, E])
        cmp2 = sb("cmp2", [P, TILES, E, E])
        cumt = sb("cumt", [P, TILES, E])
        k1 = sb("k1", [P, TILES, E])
        k2 = sb("k2", [P, TILES, E])
        gate = [sb(f"gate{h}", [P, TILES, E]) for h in range(H)]
        gates = [sb(f"gates{h}", [P, TILES, E]) for h in range(H)]
        gT = [sb(f"gT{h}", [E, TILES, P]) for h in range(H)]

        bank = [ctx.enter_context(nc.psum_tensor(f"bank{i}", [P, 512], F32)) for i in range(8)]
        tl = lambda b: bank[b][:, :].rearrange("p (t c) -> p t c", t=TILES)

        def gq(bk):
            return [bank[b][:, 0:2 * (P + 1)].rearrange("p (t c) -> p t c", t=2) for b in bk[1:3]]

        ATT = (0, 1, 2)
        ATT_FIRST = ((0, 1, 2), (4, 5, 6))
        PREP, UP, DOWN = 3, (4, 5), (6, 7)
        TURN = (3, 4)
        ZC = (3, 7)
        zc = lambda b, lo, hi: bank[ZC[b]][:, 2 * lo:2 * hi].rearrange("p (g c) -> p c g", c=2)
        sums = lambda b, k, lo, hi: bank[ZC[b]][:, 2 * G + k * (hi - lo):2 * G + (k + 1) * (hi - lo)]
        PART = ((0, B), (B, G))

        x_landed = [sem(f"x_landed{n}") for n in range(N)]
        small_landed = sem("small_landed")
        w1_landed, w2_landed = sem("w1_landed"), sem("w2_landed")
        ident_ready, tri_ready, consts = sem("ident_ready"), sem("tri_ready"), sem("consts")
        pool_link, dve_link, act_link = sem("pool_link"), sem("dve_link"), sem("act_link")
        zero_done = sem("zero_done")
        wT_ps, wT_sb = sem("wT_ps"), sem("wT_sb")
        b1T_ps, b1T_sb = sem("b1T_ps"), sem("b1T_sb")
        stats_done = sem("stats_done")
        rk_made, rkT_ps, rkT_sb, z_ps = (sem(s) for s in ("rk_made", "rkT_ps", "rkT_sb", "z_ps"))
        exp_in, exp_out = sem("exp_in"), sem("exp_out")
        ld_ready, cum_ps, cols_ready = sem("ld_ready"), sem("cum_ps"), sem("cols_ready")
        base_ready = sem("base_ready")
        scale_ready, w_squares, small_scaled = sem("scale_ready"), sem("w_squares"), sem("small_scaled")
        att = [{k: sem(f"att{h}_{k}") for k in
                ("wkx", "ldU", "wkT_ps", "wkt", "gq_ps", "B_ps", "expB", "D_ps", "dec", "rkd", "V_ps", "V", "WS_ps",
                 "R", "LT", "intra", "tmp0", "XT0", "X0_ps", "X0", "T_ps", "Tn", "XC_ps", "X", "turn_ps", "XT",
                 "last_ps", "A", "VN_ps", "vnew", "SN_ps", "S", "OT_ps", "oT", "O_ps", "x1")} for h in range(H)]
        w1_hi, w1_lo, w2_hi, w2_lo = sem("w1_hi"), sem("w1_lo"), sem("w2_hi"), sem("w2_lo")
        m = {k: sem("moe_" + k) for k in
             ("link", "xn", "xnT_ps", "xhi", "xlo", "lg_ps", "lg", "e", "gate", "gT_ps", "gT", "b2_ps", "acc0",
              "up_ps", "hf", "hhi", "hlo", "dn_ps", "acc", "stored")}

        block = ctx.enter_context(nc.Block())

        def done(n, h, per=1, k=0):
            return n * (H * per) + (h * per + k + 1)

        def nth(n, per=1, k=0):
            return n * per + (k + 1)

        col = lambda t, n, h, i: t[:, bass.ds(n * B + (TILES * h + i), 1)]
        bc = lambda a, w: a.unsqueeze(2).to_broadcast([P, TILES, w])
        xg = lambda n, h: x_all[:, bass.ds(n, 1), TILES * h:TILES * h + TILES, :].rearrange("p a b d -> p (a b) d")

        NSMALL = 10
        UNITS = E * FB
        DOWN_LAG, GATHER_LAG = FB + 1, 2 * FB + 1
        USUAL = {**{s: (s,) for s in range(5)}, 6: (5,), 7: (6,), 9: (7,), **{s + 2: (s,) for s in range(8, 27)}}
        FIRST_ROUTER = ((7, 8), (9, 10, 11), (12, 13), (14, 15), (16, 17), (18, 19, 20, 21), (22, 23, 24, 25, 26))
        LATER = {7: (0,), 8: (1, 2), 9: (3, 4), 11: (5,), 12: (6,), 13: (7,), **{s + 6: (s,) for s in range(8, 25)}, 31: (26,)}
        T_AT = [6 + 2 * k for k in range(1, LEVELS)]
        TURN_AT = [t + 2 for t in T_AT[:-1]]

        @block.sync
        def _(sp):
            sp.dma_start(x_all[:, 0, :, :], x_v[0]).then_inc(x_landed[0], 16)
            for dst, src in ((wab[:, 0:1], W_alpha.rearrange("h d -> d h")), (wab[:, 1:2], W_beta.rearrange("h d -> d h")),
                             (alog[:, :], row(A_log).to_broadcast([P, 1])), (dtb[:, :], row(dt_bias).to_broadcast([P, 1])),
                             (wrf[:, :], Wr), (br_bc[:, :], row(br).to_broadcast([P, E]))):
                sp.dma_start(dst, src).then_inc(small_landed, 16)
            for n in range(1, N):
                sp.dma_start(x_all[:, n, :, :], x_v[n]).then_inc(x_landed[n], 16)
            sp.dma_start(w1f[:, :, :], W1.rearrange("e h f -> h e f")).then_inc(w1_landed, 16)
            for e in range(E):
                sp.dma_start(w2f[:, e, :, :], W2[e].rearrange("(c p) h -> p c h", p=P)).then_inc(w2_landed, 16)
            with sp.Fori(0, N) as n:
                for h in range(H):
                    sp.wait_ge(m["acc"], 2 + done(n, h, E, E - 1))
                    sp.dma_start(out_v[:, bass.ds(n, 1), TILES * h:TILES * h + TILES, :].rearrange("p a b d -> p (a b) d"),
                                 xg(n, h)).then_inc(m["stored"], 16)
            sp.wait_ge(m["stored"], 16 * N * H)

        @block.gpsimd
        def _(pool):
            count = [0]

            def link(ins):
                count[0] += 1
                ins.then_inc(pool_link, 1)
                pool.wait_ge(pool_link, count[0])

            link(pool.memset(ident[:, :], 0.0))
            pool.affine_select(out=ident[:, :], in_=ident[:, :], compare_op=ALU.not_equal, fill=1.0, base=0,
                               pattern=[[-1, P]], channel_multiplier=1).then_inc(ident_ready, 1)
            pool.memset(rkT_all[:, :, 0:1], 0.0).then_inc(zero_done, 1)
            for h in range(H):
                pool.memset(wkx[h][:, :, 0:1], 0.0).then_inc(zero_done, 1)
            pool.memset(ones[:, :], 1.0)
            pool.memset(upto[:, :], 1.0)
            link(pool.memset(after[:, :], 1.0))
            pool.affine_select(out=upto[:, :], in_=upto[:, :], compare_op=ALU.is_ge, fill=0.0, base=0,
                               pattern=[[1, P]], channel_multiplier=-1)
            pool.affine_select(out=after[:, :], in_=after[:, :], compare_op=ALU.is_gt, fill=0.0, base=0,
                               pattern=[[-1, P]], channel_multiplier=1).then_inc(tri_ready, 1)
            pool.memset(ones_b[:, :], 1.0)
            pool.memset(after_b[:, :], 1.0)
            pool.memset(ident_b[:, :], 0.0)
            pool.memset(far_b[:, :], 0.0)
            pool.memset(ge_tri[:, :, :], 1.0)
            link(pool.memset(join[:, :, :], 0.0))
            pool.affine_select(out=ident_b[:, :], in_=ident_b[:, :], compare_op=ALU.not_equal, fill=1.0, base=0,
                               pattern=[[-1, P]], channel_multiplier=1)
            pool.affine_select(out=after_b[:, :], in_=after_b[:, :], compare_op=ALU.is_gt, fill=0.0, base=0,
                               pattern=[[-1, P]], channel_multiplier=1)
            pool.affine_select(out=far_b[:, :], in_=far_b[:, :], compare_op=ALU.is_gt, fill=-FAR, base=0,
                               pattern=[[1, P]], channel_multiplier=-1)
            pool.affine_select(out=ge_tri[:, :, :], in_=ge_tri[:, :, :], compare_op=ALU.is_ge, fill=0.0, base=0,
                               pattern=[[1, E], [-1, E]], channel_multiplier=0)
            v0 = join[:, 0, :].rearrange("p (c s) -> p c s", s=2)[:, :, 1]
            pool.affine_select(out=v0, in_=v0, compare_op=ALU.not_equal, fill=-1.0, base=0,
                               pattern=[[-2, P // 2]], channel_multiplier=1)
            for k in range(1, LEVELS):
                b = 1 << k
                v = join[:, k, :].rearrange("p (c s w) -> p c s w", s=2, w=b)[:, :, 0, :]
                link(pool.memset(v, -1.0))
                link(pool.affine_select(out=v, in_=v, compare_op=ALU.is_ge, fill=0.0, base=-b,
                                        pattern=[[-2 * b, P // (2 * b)], [0, b]], channel_multiplier=1))
                last = pool.affine_select(out=v, in_=v, compare_op=ALU.is_ge, fill=0.0, base=2 * b - 1,
                                          pattern=[[2 * b, P // (2 * b)], [0, b]], channel_multiplier=-1)
            last.then_inc(consts, 1)

            for h in range(H):
                pool.memset(S[h][:, :, :], 0.0).then_inc(zero_done, 1)

            def log_decays(n, h):
                for q in range(3):
                    ins = pool.tensor_tensor(ldU[h][:, q, :, :], upto[:, :].unsqueeze(1).to_broadcast([P, TILES, P]),
                                             bc(ldp[:, q, bass.ds(n * B + TILES * h, TILES)], P), ALU.mult)
                ins.then_inc(att[h]["ldU"], 1)

            def keys(n, h):
                a = att[h]
                pool.wait_ge(a["x1"], nth(n))
                pool.tensor_copy(wkx[h][:, :, :],
                                 rkT_all[:, TILES * h:TILES * h + TILES, bass.ds(n * P, P + 1)]).then_inc(a["wkx"], 1)
                log_decays(n, h)

            def decayed(n, h):
                pool.wait_ge(att[h]["expB"], nth(n))
                pool.tensor_tensor(rkd[h][:, :, :], wkx[h][:, :, 1:P + 1], expB[h][:, :, :],
                                   ALU.mult).then_inc(att[h]["rkd"], 1)

            def first_level(n, h):
                a = att[h]
                pool.wait_ge(a["LT"], nth(n))
                pool.tensor_tensor(Tn[h][:, :, :], LT[h][:, :, :],
                                   join[:, 0, :].unsqueeze(1).to_broadcast([P, TILES, P]), ALU.mult).then_inc(a["tmp0"], 1)
                pool.wait_ge(a["tmp0"], nth(n))
                pool.tensor_tensor(XT[h][:, :, :], Tn[h][:, :, :],
                                   ident[:, :].unsqueeze(1).to_broadcast([P, TILES, P]), ALU.add).then_inc(a["XT0"], 1)

            pool.wait_ge(ld_ready, 3)
            log_decays(0, 1)
            first_level(0, 1)
            for h in range(H):
                pool.nop().then_inc(att[h]["rkd"], 1)
            pool.wait_ge(scale_ready, 1)
            pool.partition_all_reduce(wmax[:, 4:8], wmax[:, 0:4], P, RMAX).then_inc(scale_ready, 1)
            KEYS_AFTER = 4
            for e in range(E):
                pool.wait_ge(w2_hi, 2 * e + 2)
                pool.tensor_tensor(w2p[:, 1, e, :, :], w2f[:, e, :, :], w2p[:, 0, e, :, :], ALU.subtract).then_inc(w2_lo, 1)
                if e == KEYS_AFTER:
                    pool.wait_ge(rkT_sb, N * H)
                    pool.wait_ge(ld_ready, 6)
                    keys(1, 0)
            decayed(1, 0)
            first_level(1, 0)
            with pool.Fori(0, N - 2) as n:
                for group in ((n + 1, 1), (n + 2, 0)):
                    keys(*group)
                    decayed(*group)
                    first_level(*group)
            keys(N - 1, 1)
            decayed(N - 1, 1)
            first_level(N - 1, 1)

        @block.scalar
        def _(act):
            small = [(wwf[:, :], W_write), (wof[:, :], W_read), (b2_sb[:, :], b2),
                     (b1r[:, :], b1.rearrange("e (c p) -> (e c) p", p=P))]
            assert len(small) == NSMALL - 6
            for dst, src in small:
                act.dma_start(dst, src).then_inc(small_landed, 16)

            act.wait_ge(small_landed, 16 * NSMALL)
            act.activation(nega[:, :], alog[:, :], ACT.Exp).then_inc(act_link, 1)

            act.wait_ge(wT_ps, 2)
            act.activation(WwT[:, :], bank[6][:, 0:P], ACT.Copy).then_inc(wT_sb, 1)
            act.activation(WoT[:, :], bank[6][:, P:2 * P], ACT.Copy).then_inc(wT_sb, 1)

            act.wait_ge(b1T_ps, 1)
            act.activation(b1s[:, :, :].rearrange("p e c -> p (e c)"), bank[7][:, 0:E * FB], ACT.Copy).then_inc(b1T_sb, 1)

            def keep_rkT(n, h):
                act.wait_ge(rkT_ps, done(n, h))
                src = tl(TURN[h] if n == 0 else TURN[0])
                if n == 0:
                    act.activation(wkx[h][:, :, 1:P + 1], src, ACT.Copy).then_inc(att[h]["wkx"], 1)
                first = P - 1 if n == 0 else 0
                act.activation(rkT_all[:, TILES * h:TILES * h + TILES, n * P + 1 + first:n * P + P + 1], src[:, :, first:P],
                               ACT.Copy).then_inc(rkT_sb, 1)

            def base(n, h, i):
                act.activation(xg(n, h)[:, i, :], xg(n, h)[:, i, :], ACT.Identity, scale=col(sc["one"], n, h, i),
                               bias=col(sc["nmr"], n, h, i)).then_inc(base_ready, 1)

            def gates_exp(p):
                lo, hi = PART[p]
                act.wait_ge(exp_in, 2 * p + 2)
                act.activation(s2["u"][:, :, lo:hi], s2["n"][:, :, lo:hi], ACT.Exp).then_inc(act_link, 1)
                act.activation(sc["num"][:, lo:hi], sc["mb"][:, lo:hi], ACT.Exp).then_inc(exp_out, 1)
                act.wait_ge(act_link, 2 + p)
                act.activation(sc["la"][:, lo:hi], s2["u"][:, 0, lo:hi], ACT.Ln, bias=1.0).then_inc(exp_out, 1)

            def decays_exp(p):
                lo, hi = PART[p]
                act.wait_ge(cum_ps, 3 * p + 3)
                for k, name in enumerate(("dexp", "ced", "tail")):
                    act.activation(sc[name][:, lo:hi], sums(p, k, lo, hi), ACT.Exp).then_inc(exp_out, 1)

            for h in range(H):
                keep_rkT(0, h)
            gates_exp(0)
            decays_exp(0)
            act.wait_ge(cols_ready, 1)

            def scaled(dst, bk, name, n, h):
                for i in range(TILES):
                    ins = act.activation(dst[h][:, i, :], tl(bk)[:, i, :], ACT.Copy, scale=col(sc[name], n, h, i))
                return ins

            def att_keys(n, h, bk):
                act.wait_ge(att[h]["wkT_ps"], nth(n))
                scaled(wkt, bk[0], "tail", n, h).then_inc(att[h]["wkt"], 1)

            def att_expB(n, h, bk):
                act.wait_ge(att[h]["B_ps"], nth(n))
                act.activation(expB[h][:, :, :], tl(bk[0]), ACT.Exp).then_inc(att[h]["expB"], 1)

            def att_dec(n, h, bk):
                act.wait_ge(att[h]["D_ps"], nth(n))
                act.activation(dec[h][:, :, :], tl(bk[0]), ACT.Exp).then_inc(att[h]["dec"], 1)

            def att_v(n, h, bk):
                act.wait_ge(att[h]["V_ps"], nth(n))
                scaled(V, bk[0], "nrm", n, h).then_inc(att[h]["V"], 1)

            def att_x0(n, h, bk):
                act.wait_ge(att[h]["X0_ps"], nth(n))
                act.activation(X[h][:, :, :], tl(bk[2]), ACT.Copy).then_inc(att[h]["X0"], 1)

            def att_xt(n, h, bk, k):
                act.wait_ge(att[h]["turn_ps"], nth(n, LEVELS - 2, k - 1))
                act.activation(XT[h][:, :, :], tl(bk[2]), ACT.Copy).then_inc(att[h]["XT"], 1)

            def att_vnew(n, h, bk):
                act.wait_ge(att[h]["VN_ps"], nth(n))
                scaled(vnew, bk[0], "beta", n, h).then_inc(att[h]["vnew"], 1)

            def att_oT(n, h, bk):
                act.wait_ge(att[h]["OT_ps"], nth(n))
                act.activation(oT[h][:, :, :], tl(bk[2]), ACT.Copy).then_inc(att[h]["oT"], 1)

            def weight_squares(k, i):
                half = slice(i * E * F // 2, (i + 1) * E * F // 2)
                w = w2words if k else w1f[:, :, :].rearrange("p e f -> p (e f)")
                act.wait_ge(w2_landed if k else w1_landed, 16 * (E if k else 1))
                act.activation(squares[k][:, half], w[:, half], ACT.Square,
                               accum_out=wsq[:, 2 * k + i:2 * k + i + 1]).then_inc(w_squares, 1)

            def high_1(e):
                act.activation(w1p[:, 0, e, :], w1f[:, e, :], ACT.Copy, scale=wmax[:, 4:5]).then_inc(w1_hi, 1)

            def high_2(e):
                act.activation(w2p[:, 0, e, :, :], w2f[:, e, :, :], ACT.Copy, scale=wmax[:, 5:6]).then_inc(w2_hi, 1)
                act.activation(w2f[:, e, :, :], w2f[:, e, :, :], ACT.Copy, scale=wmax[:, 5:6]).then_inc(w2_hi, 1)

            BASE_AT = (9, 11, 13, 15)

            def att_at(u, n, h):
                bk = ATT
                if u == 0:
                    att_keys(n, h, bk)
                if u == 1:
                    att_expB(n, h, bk)
                if u == 3:
                    att_dec(n, h, bk)
                if u == 4:
                    att_v(n, h, bk)
                if u == 7:
                    att_x0(n, h, bk)
                if u in TURN_AT:
                    att_xt(n, h, bk, TURN_AT.index(u) + 1)
                if u in BASE_AT:
                    base(n, h, BASE_AT.index(u))
                if u == 20:
                    att_vnew(n, h, bk)
                if u == 21:
                    att_oT(n, h, bk)

            def prep_at(u, n, h):
                if u == 5:
                    act.wait_ge(m["xnT_ps"], done(n, h))
                    act.activation(xp[h][:, 0, :, :], tl(PREP), ACT.Copy, scale=X_SCALE).then_inc(m["xhi"], 1)
                if u == 10:
                    act.wait_ge(m["lg"], done(n, h))
                    act.activation(pe_[:, :, :], lg[:, :, :], ACT.Exp).then_inc(m["e"], 1)
                if u == 22:
                    act.wait_ge(m["gT_ps"], done(n, h))
                    act.activation(gT[h][:, :, :], bank[PREP][0:E, :].rearrange("p (t c) -> p t c", t=TILES),
                                   ACT.Copy).then_inc(m["gT"], 1)

            def slot(moe, prep, attn, before):
                n, h = moe
                for u in range(UNITS):
                    e, c = divmod(u, FB)
                    act.wait_ge(m["up_ps"], done(n, h, UNITS, u))
                    act.wait_ge(m["hlo"], done(n, h, UNITS, u))
                    act.activation(hf[u % 2], bank[UP[u % 2]][:, :], ACT.Relu, bias=b1s[:, e, c:c + 1],
                                   scale=H_SCALE).then_inc(m["hf"], 1)
                    if c == 0:
                        act.wait_ge(m["dn_ps"], done(n, h, E, e))
                    act.activation(hp[e % 2][:, 0, c, :], bank[UP[u % 2]][:, :], ACT.Relu,
                                   bias=b1s[:, e, c:c + 1], scale=H_SCALE).then_inc(m["hhi"], 1)
                    if attn:
                        att_at(u, *attn)
                    if before is None:
                        for stage in FIRST_ROUTER[u] if u < len(FIRST_ROUTER) else ():
                            prep_at(stage, *moe)
                    if prep:
                        for stage in (USUAL if before else LATER).get(u, ()):
                            prep_at(stage, *prep)

            for h in range(H):
                att_keys(0, h, ATT_FIRST[h])
                act.nop().then_inc(att[h]["expB"], 1)
            att_dec(0, 0, ATT_FIRST[0])
            weight_squares(0, 0)
            att_dec(0, 1, ATT_FIRST[1])
            att_v(0, 0, ATT_FIRST[0])
            att_x0(0, 0, ATT_FIRST[0])
            att_v(0, 1, ATT_FIRST[1])
            att_x0(0, 1, ATT_FIRST[1])
            weight_squares(0, 1)
            weight_squares(1, 0)
            keep_rkT(1, 0)
            act.wait_ge(rk_made, H)
            for k in range(1, LEVELS - 1):
                for h in range(H):
                    att_xt(0, h, ATT_FIRST[h], k)
                if k == 1:
                    weight_squares(1, 1)
                    keep_rkT(1, 1)
                    keep_rkT(2, 0)
                    for i in range(TILES):
                        base(0, 0, i)
                if k == 2:
                    keep_rkT(2, 1)
                    keep_rkT(3, 0)
                    act.wait_ge(scale_ready, 3)
                    act.wait_ge(w_squares, 4)
                    high_1(0)
                    high_1(1)
                if k == 3:
                    keep_rkT(3, 1)
                    high_1(2)
                    high_2(0)
                    high_1(3)
                if k == 4:
                    gates_exp(1)
                    high_2(1)
                    high_1(4)
                    high_2(2)
                if k == 5:
                    decays_exp(1)
                    high_1(5)
            att_vnew(0, 0, ATT_FIRST[0])
            high_1(6)
            high_2(3)
            high_1(7)
            att_oT(0, 0, ATT_FIRST[0])
            att_vnew(0, 1, ATT_FIRST[1])
            for i in range(TILES):
                base(0, 1, i)
            att_oT(0, 1, ATT_FIRST[1])
            high_2(4)
            high_2(5)
            high_2(6)
            prep_at(5, 0, 0)
            high_2(7)
            act.nop().then_inc(m["hhi"], 2)
            act.wait_ge(w1_lo, E)
            act.wait_ge(w2_lo, 2)
            act.wait_ge(cols_ready, 2)
            slot((0, 0), (0, 1), (1, 0), None)
            with act.Fori(0, N - 2) as n:
                slot((n, 1), (n + 1, 0), (n + 1, 1), (n, 0))
                slot((n + 1, 0), (n + 1, 1), (n + 2, 0), (n, 1))
            slot((N - 2, 1), (N - 1, 0), (N - 1, 1), (N - 2, 0))
            slot((N - 1, 0), (N - 1, 1), None, (N - 2, 1))
            slot((N - 1, 1), None, None, (N - 1, 0))

        @block.vector
        def _(dve):
            count = [0]

            def link(ins):
                count[0] += 1
                ins.then_inc(dve_link, 1)
                dve.wait_ge(dve_link, count[0])

            def rsqrt(x, y, q, link):
                link(dve.tensor_scalar(y.bitcast(I32), x.bitcast(I32), -0.5, RSQRT_SEED, ALU.mult, ALU.add))
                for _ in range(3):
                    link(dve.scalar_tensor_tensor(q, y, -0.5, y, ALU.mult, ALU.mult))
                    link(dve.tensor_tensor(q, q, x, ALU.mult))
                    link(dve.scalar_tensor_tensor(y, q, 1.5, y, ALU.add, ALU.mult))

            def statistics(n):
                dve.wait_ge(x_landed[n], 16)
                for b in range(B):
                    dve.bn_stats(stats[:, n * B + b, :], x_all[:, n, b, :]).then_inc(stats_done, 1)

            def moments(p):
                dve.wait_ge(stats_done, PART[p][1])
                for g in range(*PART[p]):
                    last = dve.bn_aggr(mv[:, g, :], stats[:, g, :])
                link(last)

            def norms(p):
                lo, hi = PART[p]
                mean, var = mv[:, lo:hi, 0], mv[:, lo:hi, 1]
                dve.tensor_scalar(s2["v"][:, 0, lo:hi], var, LN_EPS, None, ALU.add)
                link(dve.tensor_scalar(s2["v"][:, 1, lo:hi], var, float(D), 1e-30, ALU.mult, ALU.max))
                rsqrt(s2["v"][:, :, lo:hi], s2["r"][:, :, lo:hi], s2["q"][:, :, lo:hi], link)
                rstd, rn = s2["r"][:, 0, lo:hi], s2["r"][:, 1, lo:hi]
                link(dve.scalar_tensor_tensor(sc["f"][:, lo:hi], rstd, 1e12, rn, ALU.mult, ALU.min))
                dve.tensor_scalar(sc["one"][:, lo:hi], rstd, 1.0, None, ALU.add)
                dve.scalar_tensor_tensor(sc["nmr"][:, lo:hi], mean, -1.0, rstd, ALU.mult, ALU.mult)

            def read_keys(n, h):
                if n > 0:
                    dve.wait_ge(rkT_ps, done(n - 1, h))
                for i in range(TILES):
                    g = n * B + TILES * h + i
                    ins = dve.tensor_scalar(rk[h][:, i, :], x_all[:, n, TILES * h + i, :], mv[:, g, 0:1],
                                            sc["f"][:, g:g + 1], ALU.subtract, ALU.mult)
                ins.then_inc(rk_made, 1)

            def lengths(p):
                lo, hi = PART[p]
                s = sc["nrm"][:, lo:hi]
                link(dve.tensor_tensor(s, s2["v"][:, 1, lo:hi], s2["r"][:, 1, lo:hi], ALU.mult))
                link(dve.tensor_tensor(s, s, s2["r"][:, 0, lo:hi], ALU.mult))
                link(dve.tensor_scalar(s, s, 1e-12, None, ALU.max))

            def gates_in(p):
                lo, hi = PART[p]
                z, na = s2["z"][:, :, lo:hi], s2["n"][:, :, lo:hi]
                dve.wait_ge(z_ps, PART[p][1] // TILES)
                link(dve.tensor_tensor(z, zc(p, lo, hi), sc["nrm"][:, lo:hi].unsqueeze(1).to_broadcast([P, 2, hi - lo]), ALU.mult))
                dve.wait_ge(small_landed, 16 * NSMALL)
                link(dve.tensor_scalar(s2["z"][:, 0, lo:hi], s2["z"][:, 0, lo:hi], dtb[:, :], None, ALU.add))
                dve.scalar_tensor_tensor(na, z, -1.0, z, ALU.mult, ALU.min).then_inc(exp_in, 1)
                dve.tensor_scalar(sc["mb"][:, lo:hi], s2["z"][:, 1, lo:hi], 0.0, None, ALU.min).then_inc(exp_in, 1)

            def gates_out(p):
                lo, hi = PART[p]
                s = {k: t[:, lo:hi] for k, t in sc.items()}
                dve.wait_ge(exp_out, 5 * p + 2)
                link(dve.scalar_tensor_tensor(s["la"], s2["z"][:, 0, lo:hi], 0.0, s["la"], ALU.max, ALU.add))
                if p == 0:
                    dve.wait_ge(act_link, 1)
                    link(dve.tensor_scalar(nega[:, :], nega[:, :], -1.0, None, ALU.mult))
                dve.tensor_scalar(s["ld"], s["la"], nega[:, :], None, ALU.mult).then_inc(ld_ready, 1)
                dve.tensor_scalar(ldp[:, 0, lo:hi], s["la"], nega[:, :], None, ALU.mult).then_inc(ld_ready, 1)
                dve.wait_ge(ld_ready, 3 * p + 2)
                link(dve.tensor_tensor(s["ldr"], s["ld"], ldp[:, 0, lo:hi], ALU.subtract))
                link(dve.tensor_copy(ldp[:, 1, lo:hi], s["ldr"]))
                link(dve.tensor_tensor(ldp[:, 2, lo:hi], s["ldr"], ldp[:, 1, lo:hi], ALU.subtract))
                dve.nop().then_inc(ld_ready, 1)
                link(dve.tensor_scalar(s["den"], s2["u"][:, 1, lo:hi], 1.0, None, ALU.add))
                link(dve.reciprocal(s["den"], s["den"]))
                link(dve.tensor_tensor(s["beta"], s["den"], s["num"], ALU.mult))

            def decays_out(p):
                lo, hi = PART[p]
                dve.wait_ge(exp_out, 5 * p + 5)
                dve.tensor_scalar(sc["ndexp"][:, lo:hi], sc["dexp"][:, lo:hi], -1.0, None, ALU.mult).then_inc(cols_ready, 1)

            def weight_bounds():
                dve.wait_ge(w_squares, 4)
                dve.tensor_reduce(wmax[:, 0:2], wsq[:, :].rearrange("p (w i) -> p w i", w=2), AX_X, ALU.max)
                dve.wait_ge(b1T_sb, 1)
                for k, t in ((2, wrf[:, :]), (3, b1s[:, :, :].rearrange("p e c -> p (e c)"))):
                    last = dve.tensor_reduce(wmax[:, k:k + 1], t, AX_X, ALU.max, apply_absolute_value=True)
                last.then_inc(scale_ready, 1)

            def weight_scales():
                dve.wait_ge(scale_ready, 2)
                link(dve.tensor_scalar(wmax[:, 4:8], wmax[:, 4:8], 1e-30, None, ALU.max))
                link(dve.tensor_scalar(wmax[:, 4:6].bitcast(I32), wmax[:, 4:6].bitcast(I32), 0.5, float(0x3F800000 // 2),
                                       ALU.mult, ALU.add))
                link(dve.scalar_tensor_tensor(wmax[:, 4:5], wmax[:, 4:5], float(P), wmax[:, 7:8], ALU.mult, ALU.add))
                link(dve.tensor_scalar(wmax[:, 4:7].bitcast(I32), wmax[:, 4:7].bitcast(I32), 0x7F800000, None, ALU.bitwise_and))
                link(dve.reciprocal(wmax[:, 4:7], wmax[:, 4:7]))
                link(dve.tensor_scalar(wmax[:, 4:5], wmax[:, 4:5], 2.0 ** 14 / (X_SCALE * H_SCALE), None, ALU.mult))
                link(dve.tensor_scalar(wmax[:, 5:7], wmax[:, 5:7], 2.0 ** 12, None, ALU.mult))
                dve.nop().then_inc(scale_ready, 1)

            def weight_small():
                b1c = b1s[:, :, :].rearrange("p e c -> p (e c)")
                dve.tensor_scalar(wmax[:, 0:1], wmax[:, 6:7], X_SCALE, None, ALU.mult)
                link(dve.scalar_tensor_tensor(wmax[:, 1:2], wmax[:, 4:5], X_SCALE * H_SCALE, wmax[:, 5:6], ALU.mult, ALU.mult))
                link(dve.reciprocal(wmax[:, 0:2], wmax[:, 0:2]))
                dve.tensor_scalar(b1c, b1c, wmax[:, 4:5], X_SCALE * H_SCALE, ALU.mult, ALU.mult).then_inc(small_scaled, 1)
                link(dve.tensor_scalar(wrp[:, 0, :], wrf[:, :], wmax[:, 6:7], None, ALU.mult))
                dve.scalar_tensor_tensor(wrp[:, 1, :], wrf[:, :], wmax[:, 6:7], wrp[:, 0, :], ALU.mult,
                                         ALU.subtract).then_inc(small_scaled, 1)

            def att_products(n, h, bk):
                a = att[h]
                dve.wait_ge(a["gq_ps"], nth(n))
                dve.wait_ge(a["dec"], nth(n))
                for i in range(TILES):
                    ins = dve.scalar_tensor_tensor(LT[h][:, i, :], gq(bk)[i // 2][:, i % 2, 0:P], col(sc["beta"], n, h, i),
                                                   dec[h][:, i, :], ALU.mult, ALU.mult)
                ins.then_inc(a["LT"], 1)
                for c in range(2):
                    ins = dve.tensor_tensor(intraT[h][:, 2 * c:2 * c + 2, :], gq(bk)[c][:, :, 1:P + 1],
                                            dec[h][:, 2 * c:2 * c + 2, :], ALU.mult)
                ins.then_inc(a["intra"], 1)

            def att_r(n, h, bk):
                a = att[h]
                dve.wait_ge(a["WS_ps"], nth(n))
                dve.wait_ge(a["V"], nth(n))
                for i in range(TILES):
                    ins = dve.scalar_tensor_tensor(R[h][:, i, :], tl(bk[1])[:, i, :], col(sc["ndexp"], n, h, i),
                                                   V[h][:, i, :], ALU.mult, ALU.add)
                ins.then_inc(a["R"], 1)

            def att_tn(n, h, bk, k):
                a = att[h]
                dve.wait_ge(a["T_ps"], nth(n, LEVELS - 1, k - 1))
                dve.tensor_tensor(Tn[h][:, :, :], tl(bk[0]), join[:, k, :].unsqueeze(1).to_broadcast([P, TILES, P]),
                                  ALU.mult).then_inc(a["Tn"], 1)

            def att_x(n, h, bk, k):
                a = att[h]
                if k < LEVELS - 1:
                    dve.wait_ge(a["XC_ps"], nth(n, LEVELS - 2, k - 1))
                    dve.tensor_tensor(X[h][:, :, :], tl(bk[1]), X[h][:, :, :], ALU.add).then_inc(a["X"], 1)
                else:
                    dve.wait_ge(a["last_ps"], nth(n))
                    dve.tensor_tensor(XT[h][:, :, :], tl(bk[1]), XT[h][:, :, :], ALU.add).then_inc(a["A"], 1)

            def att_s(n, h, bk):
                a = att[h]
                dve.wait_ge(a["SN_ps"], nth(n))
                dve.wait_ge(a["OT_ps"], nth(n))
                for i in range(TILES):
                    ins = dve.scalar_tensor_tensor(S[h][:, i, :], S[h][:, i, :], col(sc["ced"], n, h, i),
                                                   tl(bk[1])[:, i, :], ALU.mult, ALU.add)
                ins.then_inc(a["S"], 1)

            def att_x1(n, h, bk):
                dve.wait_ge(att[h]["O_ps"], nth(n))
                dve.wait_ge(base_ready, done(n, h, TILES, TILES - 1))
                dve.tensor_tensor(xg(n, h), tl(bk[0]), xg(n, h), ALU.add).then_inc(att[h]["x1"], 1)

            def split_low(e):
                dve.wait_ge(w1_hi, e + 1)
                dve.scalar_tensor_tensor(w1p[:, 1, e, :], w1f[:, e, :], wmax[:, 4:5], w1p[:, 0, e, :], ALU.mult,
                                         ALU.subtract).then_inc(w1_lo, 1)

            def att_at(u, n, h):
                bk = ATT
                if u == 4:
                    att_products(n, h, bk)
                if u == 6:
                    att_r(n, h, bk)
                if u in T_AT:
                    att_tn(n, h, bk, T_AT.index(u) + 1)
                if u - 1 in T_AT:
                    att_x(n, h, bk, T_AT.index(u - 1) + 1)
                if u == 22:
                    att_s(n, h, bk)
                if u == 23:
                    att_x1(n, h, bk)

            LINKS = 40
            r = {k: t[:, :] for k, t in mr_.items()}
            pj = pr[:, :, :].unsqueeze(2).to_broadcast([P, TILES, E, E])
            pe = pr[:, :, :].unsqueeze(3).to_broadcast([P, TILES, E, E])
            tri = ge_tri[:, :, :].unsqueeze(1).to_broadcast([P, TILES, E, E])
            cnt = [0]

            def prep_at(u, n, h):
                if u == 0:
                    cnt[0] = 0

                def mlink(ins):
                    cnt[0] += 1
                    ins.then_inc(m["link"], 1)

                def prior():
                    dve.wait_ge(m["link"], n * (H * LINKS) + (h * LINKS + cnt[0]))

                if u == 0:
                    dve.wait_ge(att[h]["x1"], 1 + nth(n))
                    dve.sem_inc(m["link"], 1)
                    cnt[0] += 1
                    for i in range(TILES):
                        last = dve.bn_stats(mst[:, i, :], xg(n, h)[:, i, :])
                    mlink(last)
                if u == 1:
                    prior()
                    dve.sem_inc(m["link"], 1)
                    cnt[0] += 1
                    for i in range(TILES):
                        last = dve.bn_aggr(mmv[:, i, :], mst[:, i, :])
                    mlink(last)
                    prior()
                    mlink(dve.tensor_scalar(r["ve"], mmv[:, :, 1], LN_EPS, None, ALU.add))
                if u == 2:
                    prior()
                    mlink(dve.tensor_scalar(r["r"].bitcast(I32), r["ve"].bitcast(I32), -0.5, RSQRT_SEED, ALU.mult, ALU.add))
                if u in (2, 3, 4):
                    prior()
                    mlink(dve.scalar_tensor_tensor(r["q"], r["r"], -0.5, r["r"], ALU.mult, ALU.mult))
                    prior()
                    mlink(dve.tensor_tensor(r["q"], r["q"], r["ve"], ALU.mult))
                    prior()
                    mlink(dve.scalar_tensor_tensor(r["r"], r["q"], 1.5, r["r"], ALU.add, ALU.mult))
                if u == 4:
                    prior()
                    for i in range(TILES):
                        last = dve.tensor_scalar(xn[h][:, i, :], xg(n, h)[:, i, :], mmv[:, i, 0:1], mr_["r"][:, i:i + 1],
                                                 ALU.subtract, ALU.mult)
                    last.then_inc(m["xn"], 1)
                if u == 6:
                    dve.wait_ge(m["xhi"], done(n, h))
                    dve.scalar_tensor_tensor(xp[h][:, 1, :, :], tl(PREP), X_SCALE, xp[h][:, 0, :, :], ALU.mult,
                                             ALU.subtract).then_inc(m["xlo"], 1)
                if u == 8:
                    dve.wait_ge(m["lg_ps"], done(n, h))
                    parts = bank[PREP][:, 0:2 * TILES * E].rearrange("p (t w e) -> p t w e", w=2, e=E)
                    mlink(dve.scalar_tensor_tensor(lg[:, :, :], parts[:, :, 1, :], wmax[:, 0:1],
                                                   br_bc[:, :].unsqueeze(1).to_broadcast([P, TILES, E]), ALU.mult, ALU.add))
                    prior()
                    mlink(dve.scalar_tensor_tensor(lg[:, :, :], parts[:, :, 0, :], wmax[:, 0:1], lg[:, :, :],
                                                   ALU.mult, ALU.add))
                    prior()
                    mlink(dve.tensor_reduce(r["mx"], lg[:, :, :], AX_X, ALU.max))
                if u == 9:
                    prior()
                    dve.tensor_tensor(lg[:, :, :], lg[:, :, :], bc(r["mx"], E), ALU.subtract).then_inc(m["lg"], 1)
                if u == 11:
                    dve.wait_ge(m["e"], done(n, h))
                    mlink(dve.tensor_reduce(r["sum"], pe_[:, :, :], AX_X, ALU.add))
                    prior()
                    mlink(dve.reciprocal(r["rs"], r["sum"]))
                if u == 12:
                    prior()
                    mlink(dve.tensor_tensor(pr[:, :, :], pe_[:, :, :], bc(r["rs"], E), ALU.mult))
                if u == 13:
                    prior()
                    mlink(dve.tensor_tensor(cmp1[:, :, :, :], pj, pe, ALU.is_ge))
                    mlink(dve.tensor_tensor(cmp2[:, :, :, :], pj, pe, ALU.is_gt))
                if u == 14:
                    prior()
                    mlink(dve.tensor_tensor(cmp1[:, :, :, :], cmp1[:, :, :, :], tri, ALU.mult))
                if u == 15:
                    prior()
                    mlink(dve.tensor_tensor(cmp1[:, :, :, :], cmp1[:, :, :, :], cmp2[:, :, :, :], ALU.max))
                if u == 16:
                    prior()
                    mlink(dve.tensor_tensor(cmp1[:, :, :, :], cmp1[:, :, :, :], pj, ALU.mult))
                if u == 17:
                    prior()
                    mlink(dve.tensor_reduce(cumt[:, :, :], cmp1[:, :, :, :], AX_X, ALU.add))
                if u == 18:
                    prior()
                    mlink(dve.tensor_scalar(k1[:, :, :], cumt[:, :, :], TOP_P, None, ALU.is_lt))
                    mlink(dve.tensor_tensor(k2[:, :, :], cumt[:, :, :], pr[:, :, :], ALU.is_le))
                if u == 19:
                    prior()
                    mlink(dve.tensor_tensor(k1[:, :, :], k1[:, :, :], k2[:, :, :], ALU.max))
                if u == 20:
                    prior()
                    dve.tensor_tensor(gate[h][:, :, :], pr[:, :, :], k1[:, :, :], ALU.mult).then_inc(m["gate"], 1)
                if u == 21:
                    dve.wait_ge(m["gate"], done(n, h))
                    mlink(dve.tensor_scalar(gates[h][:, :, :], gate[h][:, :, :], wmax[:, 1:2], None, ALU.mult))
                if u == 26:
                    prior()
                    dve.wait_ge(m["b2_ps"], done(n, h))
                    dve.tensor_tensor(xg(n, h), tl(PREP), xg(n, h), ALU.add).then_inc(m["acc0"], 1)
                    assert cnt[0] <= LINKS
                    if cnt[0] < LINKS:
                        dve.nop().then_inc(m["link"], LINKS - cnt[0])

            def gather(group, e, i):
                n, h = group
                if i == 0:
                    dve.wait_ge(m["dn_ps"], 2 + done(n, h, E, e))
                    if e == 0:
                        dve.wait_ge(m["acc0"], done(n, h))
                    else:
                        dve.wait_ge(m["acc"], 2 + done(n, h, E, e - 1))
                ins = dve.scalar_tensor_tensor(xg(n, h)[:, i, :], tl(DOWN[e % 2])[:, i, :], gates[h][:, i, e:e + 1],
                                               xg(n, h)[:, i, :], ALU.mult, ALU.add)
                if i == TILES - 1:
                    ins.then_inc(m["acc"], 1)

            def slot(moe, prep, attn, before):
                n, h = moe
                for u in range(UNITS):
                    e, c = divmod(u, FB)
                    if u >= GATHER_LAG:
                        gather(moe, *divmod(u - GATHER_LAG, TILES))
                    elif before:
                        gather(before, *divmod(UNITS + u - GATHER_LAG, TILES))
                    if attn:
                        att_at(u, *attn)
                    dve.wait_ge(m["hf"], done(n, h, UNITS, u))
                    dve.wait_ge(m["hhi"], 2 + done(n, h, UNITS, u))
                    dve.tensor_tensor(hp[e % 2][:, 1, c, :], hf[u % 2], hp[e % 2][:, 0, c, :],
                                      ALU.subtract).then_inc(m["hlo"], 1)
                    if before is None:
                        for stage in FIRST_ROUTER[u] if u < len(FIRST_ROUTER) else ():
                            prep_at(stage, *moe)
                    if prep:
                        for stage in (USUAL if before else LATER).get(u, ()):
                            prep_at(stage, *prep)

            for h in range(H):
                dve.nop().then_inc(att[h]["x1"], 1)
            statistics(0)
            moments(0)
            norms(0)
            for h in range(H):
                read_keys(0, h)
            lengths(0)
            statistics(1)
            gates_in(0)
            statistics(2)
            gates_out(0)
            dve.wait_ge(tri_ready, 1)
            for q in range(3):
                ins = dve.tensor_tensor(ldU[0][:, q, :, :], upto[:, :].unsqueeze(1).to_broadcast([P, TILES, P]),
                                        bc(ldp[:, q, 0:TILES], P), ALU.mult)
            ins.then_inc(att[0]["ldU"], 1)
            decays_out(0)
            statistics(3)
            moments(1)

            dve.wait_ge(zero_done, 1 + H + H)
            for h in range(H):
                dve.nop().then_inc(att[h]["S"], 1)

            def between(k, part):
                if k <= 3:
                    read_keys(k, part)
                if (k, part) == (2, 0):
                    weight_bounds()
                if (k, part) == (2, 1):
                    weight_scales()
                if (k, part) == (3, 0):
                    weight_small()
                if (k, part) == (4, 0):
                    lengths(1)
                if (k, part) == (4, 1):
                    gates_in(1)
                if (k, part) == (5, 1):
                    gates_out(1)
                if (k, part) in ((4, 0), (4, 1), (5, 0), (6, 0)):
                    split_low(2 * (k - 4) + part - (k == 6))
                if (k, part) == (6, 1):
                    for e in range(4, 7):
                        split_low(e)

            att_products(0, 0, ATT_FIRST[0])
            dve.wait_ge(att[0]["LT"], 1)
            dve.wait_ge(consts, 1)
            dve.tensor_tensor(Tn[0][:, :, :], LT[0][:, :, :], join[:, 0, :].unsqueeze(1).to_broadcast([P, TILES, P]),
                              ALU.mult).then_inc(att[0]["tmp0"], 1)
            dve.wait_ge(att[0]["tmp0"], 1)
            dve.tensor_tensor(XT[0][:, :, :], Tn[0][:, :, :], ident[:, :].unsqueeze(1).to_broadcast([P, TILES, P]),
                              ALU.add).then_inc(att[0]["XT0"], 1)
            att_products(0, 1, ATT_FIRST[1])
            for h in range(H):
                dve.nop().then_inc(att[h]["R"], 1)
            for k in range(1, LEVELS):
                att_tn(0, 0, ATT_FIRST[0], k)
                if k == 1:
                    norms(1)
                att_tn(0, 1, ATT_FIRST[1], k)
                between(k, 0)
                for h in range(H):
                    att_x(0, h, ATT_FIRST[h], k)
                between(k, 1)
            att_s(0, 0, ATT_FIRST[0])
            decays_out(1)
            split_low(7)
            att_x1(0, 0, ATT_FIRST[0])
            for u in range(5):
                prep_at(u, 0, 0)
            att_s(0, 1, ATT_FIRST[1])
            att_x1(0, 1, ATT_FIRST[1])
            prep_at(6, 0, 0)
            dve.nop().then_inc(m["hlo"], 2)
            dve.nop().then_inc(m["acc"], 2)
            slot((0, 0), (0, 1), (1, 0), None)
            with dve.Fori(0, N - 2) as n:
                slot((n, 1), (n + 1, 0), (n + 1, 1), (n, 0))
                slot((n + 1, 0), (n + 1, 1), (n + 2, 0), (n, 1))
            slot((N - 2, 1), (N - 1, 0), (N - 1, 1), (N - 2, 0))
            slot((N - 1, 0), (N - 1, 1), None, (N - 2, 1))
            slot((N - 1, 1), None, None, (N - 1, 0))
            for q in range(UNITS - GATHER_LAG, UNITS):
                gather((N - 1, 1), *divmod(q, TILES))

        @block.tensor
        def _(pe):
            def turn_rk(n, h):
                pe.wait_ge(rk_made, done(n, h))
                if n > 0:
                    pe.wait_ge(rkT_sb, n * H + h)
                for i in range(TILES):
                    ins = pe.transpose(tl(TURN[h] if n == 0 else TURN[0])[:, i, :], rk[h][:, i, :], ident[:, :])
                ins.then_inc(rkT_ps, 1)

            def alpha_beta(n, h):
                pe.wait_ge(rkT_sb, done(n, h))
                for i in range(TILES):
                    g = n * B + TILES * h + i
                    keys = rkT_all[:, TILES * h + i, n * P + 1:n * P + P + 1] if n else wkx[h][:, i, 1:P + 1]
                    ins = pe.matmul(bank[ZC[min(n, 1)]][:, 2 * g:2 * g + 2], keys, wab[:, :], start=True, stop=True)
                ins.then_inc(z_ps, 1)

            def decay_sums(p):
                lo, hi = PART[p]
                pe.wait_ge(ld_ready, 3 * p + 1)
                for k, t in enumerate((upto, ones, after)):
                    pe.matmul(sums(p, k, lo, hi), t[:, :], sc["ld"][:, lo:hi], start=True, stop=True).then_inc(cum_ps, 1)

            pe.wait_ge(ident_ready, 1)
            pe.wait_ge(small_landed, 16 * NSMALL)
            pe.transpose(bank[6][:, 0:P], wwf[:, :], ident[:, :]).then_inc(wT_ps, 1)
            pe.transpose(bank[6][:, P:2 * P], wof[:, :], ident[:, :]).then_inc(wT_ps, 1)
            pe.transpose(bank[7][:, 0:E * FB], b1r[:, :], ident[0:E * FB, 0:E * FB]).then_inc(b1T_ps, 1)
            for h in range(H):
                turn_rk(0, h)
            for h in range(H):
                alpha_beta(0, h)
            pe.wait_ge(tri_ready, 1)
            pe.wait_ge(zero_done, 1 + H)

            def att_keys(n, h, bk):
                a = att[h]
                pe.wait_ge(a["x1"], nth(n))
                pe.wait_ge(a["wkx"], nth(n))
                for i in range(TILES):
                    ins = pe.transpose(tl(bk[0])[:, i, :], wkx[h][:, i, 0:P], ident[:, :])
                ins.then_inc(a["wkT_ps"], 1)

            def att_b(n, h, bk):
                a = att[h]
                pe.wait_ge(a["ldU"], nth(n))
                pe.wait_ge(a["wkt"], nth(n))
                for q in range(3):
                    ins = pe.matmul(bank[bk[0]][:, :], ones_b[:, :], ldU[h][:, q, :, :].rearrange("p t c -> p (t c)"),
                                    start=(q == 0), stop=(q == 2))
                ins.then_inc(a["B_ps"], 1)

            def att_gq(n, h, bk):
                for i in range(TILES):
                    ins = pe.matmul(gq(bk)[i // 2][:, i % 2, :], wkx[h][:, i, 0:P], wkx[h][:, i, :], start=True, stop=True)
                ins.then_inc(att[h]["gq_ps"], 1)

            def att_d(n, h, bk, first=False):
                a = att[h]
                if first:
                    pe.wait_ge(a["ldU"], nth(n))
                    pe.wait_ge(a["wkt"], nth(n))
                else:
                    pe.wait_ge(a["expB"], nth(n))
                for q in range(3):
                    pe.matmul(bank[bk[0]][:, :], after_b[:, :], ldU[h][:, q, :, :].rearrange("p t c -> p (t c)"),
                              start=(q == 0), stop=False)
                pe.matmul(bank[bk[0]][:, :], ident_b[:, :], far_b[:, :].unsqueeze(1).to_broadcast([P, TILES, P]),
                          start=False, stop=True).then_inc(a["D_ps"], 1)

            def att_v(n, h, bk):
                a = att[h]
                pe.wait_ge(a["dec"], nth(n))
                for i in range(TILES):
                    ins = pe.matmul(tl(bk[0])[:, i, :], wkx[h][:, i, 1:P + 1], WwT[:, :], start=True, stop=True)
                ins.then_inc(a["V_ps"], 1)

            def att_ws(n, h, bk):
                a = att[h]
                pe.wait_ge(a["intra"], nth(n))
                pe.wait_ge(a["S"], nth(n))
                for i in range(TILES):
                    ins = pe.matmul(tl(bk[1])[:, i, :], wkx[h][:, i, 0:P], S[h][:, i, :], start=True, stop=True)
                ins.then_inc(a["WS_ps"], 1)

            def att_x0(n, h, bk, first=False):
                a = att[h]
                if first:
                    pe.wait_ge(a["intra"], nth(n))
                pe.wait_ge(a["XT0"], nth(n))
                for i in range(TILES):
                    ins = pe.transpose(tl(bk[2])[:, i, :], XT[h][:, i, :], ident[:, :])
                ins.then_inc(a["X0_ps"], 1)

            def att_t(n, h, bk, k):
                a = att[h]
                if k == 1:
                    pe.wait_ge(a["X0"], nth(n))
                    pe.wait_ge(a["V"], nth(n))
                else:
                    pe.wait_ge(a["X"], nth(n, LEVELS - 2, k - 2))
                for i in range(TILES):
                    ins = pe.matmul(tl(bk[0])[:, i, :], LT[h][:, i, :], X[h][:, i, :], start=True, stop=True)
                ins.then_inc(a["T_ps"], 1)

            def att_turn(n, h, bk, k):
                for i in range(TILES):
                    ins = pe.transpose(tl(bk[2])[:, i, :], X[h][:, i, :], ident[:, :])
                ins.then_inc(att[h]["turn_ps"], 1)

            def att_xc(n, h, bk, k):
                a = att[h]
                pe.wait_ge(a["Tn"], nth(n, LEVELS - 1, k - 1))
                if k == 1:
                    pe.wait_ge(a["R"], nth(n))
                else:
                    pe.wait_ge(a["XT"], nth(n, LEVELS - 2, k - 2))
                for i in range(TILES):
                    if k < LEVELS - 1:
                        ins = pe.matmul(tl(bk[1])[:, i, :], XT[h][:, i, :], Tn[h][:, i, :], start=True, stop=True)
                    else:
                        ins = pe.matmul(tl(bk[1])[:, i, :], Tn[h][:, i, :], XT[h][:, i, :], start=True, stop=True)
                ins.then_inc(a["XC_ps"] if k < LEVELS - 1 else a["last_ps"], 1)

            def att_vn(n, h, bk, first=False):
                a = att[h]
                pe.wait_ge(a["A"], nth(n))
                r = V if first else R
                for i in range(TILES):
                    ins = pe.matmul(tl(bk[0])[:, i, :], XT[h][:, i, :], r[h][:, i, :], start=True, stop=True)
                ins.then_inc(a["VN_ps"], 1)

            def att_so(n, h, bk, first=False):
                a = att[h]
                pe.wait_ge(a["vnew"], nth(n))
                if not first:
                    pe.wait_ge(a["rkd"], nth(n))
                for i in range(TILES):
                    ins = pe.matmul(tl(bk[1])[:, i, :], wkt[h][:, i, :], vnew[h][:, i, :], start=True, stop=True)
                ins.then_inc(a["SN_ps"], 1)
                for i in range(TILES):
                    if not first:
                        pe.matmul(tl(bk[2])[:, i, :], S[h][:, i, :], rkd[h][:, i, :], start=True, stop=False)
                    ins = pe.matmul(tl(bk[2])[:, i, :], vnew[h][:, i, :], intraT[h][:, i, :], start=first, stop=True)
                ins.then_inc(a["OT_ps"], 1)

            def att_o(n, h, bk):
                a = att[h]
                pe.wait_ge(a["oT"], nth(n))
                for i in range(TILES):
                    ins = pe.matmul(tl(bk[0])[:, i, :], oT[h][:, i, :], WoT[:, :], start=True, stop=True)
                ins.then_inc(a["O_ps"], 1)

            def att_at(u, n, h):
                bk = ATT
                for at, stage in ((0, att_keys), (1, att_b), (2, att_gq), (3, att_d), (4, att_v), (5, att_ws), (7, att_x0),
                                  (20, att_vn), (21, att_so), (23, att_o)):
                    if u == at:
                        stage(n, h, bk)
                if u in T_AT:
                    att_t(n, h, bk, T_AT.index(u) + 1)
                if u in TURN_AT:
                    att_turn(n, h, bk, TURN_AT.index(u) + 1)
                if u - 1 in T_AT:
                    att_xc(n, h, bk, T_AT.index(u - 1) + 1)

            def prep_at(u, n, h):
                if u == 5:
                    pe.wait_ge(m["xn"], done(n, h))
                    for i in range(TILES):
                        ins = pe.transpose(tl(PREP)[:, i, :], xn[h][:, i, :], ident[:, :])
                    ins.then_inc(m["xnT_ps"], 1)
                if u == 7:
                    pe.wait_ge(m["xlo"], done(n, h))
                    for i in range(TILES):
                        for a in range(2):
                            ins = pe.matmul(bank[PREP][:, 2 * E * i:2 * E * i + 2 * E], xp[h][:, a, i, :],
                                            wrp[:, :, :].rearrange("p w e -> p (w e)"), start=(a == 0), stop=(a == 1))
                    ins.then_inc(m["lg_ps"], 1)
                if u == 22:
                    pe.wait_ge(m["gate"], done(n, h))
                    for i in range(TILES):
                        ins = pe.transpose(bank[PREP][0:E, i * P:(i + 1) * P], gate[h][:, i, :], ident[:, :])
                    ins.then_inc(m["gT_ps"], 1)
                if u == 24:
                    pe.wait_ge(m["gT"], done(n, h))
                    for i in range(TILES):
                        ins = pe.matmul(tl(PREP)[:, i, :], gT[h][:, i, :], b2_sb[:, :], start=True, stop=True)
                    ins.then_inc(m["b2_ps"], 1)

            def down(group, e, i):
                n, h = group
                if i == 0:
                    pe.wait_ge(m["hlo"], 2 + done(n, h, UNITS, e * FB + FB - 1))
                    pe.wait_ge(m["acc"], done(n, h, E, e))
                for c in range(FB):
                    for j, (a, w) in enumerate(((0, 0), (0, 1), (1, 0))):
                        ins = pe.matmul(tl(DOWN[e % 2])[:, i, :], hp[e % 2][:, a, c, i * P:(i + 1) * P],
                                        w2p[:, w, e, c, :], start=(c == 0 and j == 0),
                                        stop=(c == FB - 1 and j == 2))
                if i == TILES - 1:
                    ins.then_inc(m["dn_ps"], 1)

            def slot(moe, prep, attn, before):
                n, h = moe

                def up(u):
                    e, c = divmod(u, FB)
                    pe.wait_ge(m["hhi"], done(n, h, UNITS, u))
                    for j, (a, w) in enumerate(((0, 0), (1, 0), (0, 1))):
                        ins = pe.matmul(bank[UP[u % 2]][:, :], w1p[:, w, e, c * P:(c + 1) * P],
                                        xp[h][:, a, :, :].rearrange("p t c -> p (t c)"), start=(j == 0), stop=(j == 2))
                    ins.then_inc(m["up_ps"], 1)

                for u in range(UNITS):
                    e, c = divmod(u, FB)
                    up(u)
                    if before is None and u == DOWN_LAG:
                        pe.wait_ge(w2_lo, E)
                    if u >= DOWN_LAG:
                        down(moe, *divmod(u - DOWN_LAG, TILES))
                    elif before:
                        down(before, *divmod(UNITS + u - DOWN_LAG, TILES))
                    if attn:
                        att_at(u, *attn)
                    if before is None:
                        for stage in FIRST_ROUTER[u] if u < len(FIRST_ROUTER) else ():
                            prep_at(stage, *moe)
                    if prep:
                        for stage in (USUAL if before else LATER).get(u, ()):
                            prep_at(stage, *prep)

            for stage in (att_keys, att_gq):
                for h in range(H):
                    stage(0, h, ATT_FIRST[h])
            decay_sums(0)
            pe.wait_ge(consts, 1)
            pe.wait_ge(cols_ready, 1)
            for h in range(H):
                pe.nop().then_inc(att[h]["B_ps"], 1)
                pe.nop().then_inc(att[h]["WS_ps"], 1)
                att_d(0, h, ATT_FIRST[h], first=True)
            for h in range(H):
                att_v(0, h, ATT_FIRST[h])

            def between(k, part):
                if (k, part) == (1, 1):
                    turn_rk(1, 0)
                if (k, part) == (2, 0):
                    alpha_beta(1, 0)
                    turn_rk(1, 1)
                if (k, part) == (2, 1):
                    alpha_beta(1, 1)
                    turn_rk(2, 0)
                if (k, part) == (3, 0):
                    alpha_beta(2, 0)
                    turn_rk(2, 1)
                if (k, part) == (3, 1):
                    alpha_beta(2, 1)
                    turn_rk(3, 0)
                if (k, part) == (4, 0):
                    alpha_beta(3, 0)
                    turn_rk(3, 1)
                if (k, part) == (4, 1):
                    alpha_beta(3, 1)
                if (k, part) == (6, 0):
                    decay_sums(1)

            for k in range(1, LEVELS):
                for h in range(H):
                    if k == 1:
                        att_x0(0, h, ATT_FIRST[h], first=True)
                    att_t(0, h, ATT_FIRST[h], k)
                    if k > 1:
                        att_turn(0, h, ATT_FIRST[h], k - 1)
                between(k, 0)
                for h in range(H):
                    att_xc(0, h, ATT_FIRST[h], k)
                between(k, 1)
            att_vn(0, 0, ATT_FIRST[0], first=True)
            att_so(0, 0, ATT_FIRST[0], first=True)
            att_vn(0, 1, ATT_FIRST[1], first=True)
            att_o(0, 0, ATT_FIRST[0])
            att_so(0, 1, ATT_FIRST[1], first=True)
            att_o(0, 1, ATT_FIRST[1])
            pe.wait_ge(small_scaled, 2)
            prep_at(5, 0, 0)
            pe.wait_ge(m["xlo"], 1)
            for h in range(H):
                pe.wait_ge(att[h]["x1"], 1 + nth(0))
            pe.wait_ge(w1_lo, E)
            pe.wait_ge(cols_ready, 2)
            pe.nop().then_inc(m["dn_ps"], 2)
            slot((0, 0), (0, 1), (1, 0), None)
            with pe.Fori(0, N - 2) as n:
                slot((n, 1), (n + 1, 0), (n + 1, 1), (n, 0))
                slot((n + 1, 0), (n + 1, 1), (n + 2, 0), (n, 1))
            slot((N - 2, 1), (N - 1, 0), (N - 1, 1), (N - 2, 0))
            slot((N - 1, 0), (N - 1, 1), None, (N - 2, 1))
            slot((N - 1, 1), None, None, (N - 1, 0))
            for q in range(UNITS - DOWN_LAG, UNITS):
                down((N - 1, 1), *divmod(q, TILES))


_INS = ['L0_attn_out', 'L0_attn_W_write', 'L0_attn_W_read', 'L0_attn_W_alpha', 'L0_attn_W_beta', 'L0_attn_A_log',
        'L0_attn_dt_bias', 'L0_ffn_Wr', 'L0_ffn_br', 'L0_ffn_W1', 'L0_ffn_b1', 'L0_ffn_W2', 'L0_ffn_b2']


def kernel(**inputs):
    import numpy as _np
    import concourse.bacc as _bacc
    from concourse import mybir as _mybir
    from concourse.bass_utils import run_bass_kernel_spmd as _run

    nc = _bacc.Bacc("TRN2", target_bir_lowering=False, num_devices=1)
    arrays, args = {}, []
    for name in _INS:
        a = _np.ascontiguousarray(inputs[name])
        arrays[f"in_{name}_dram"] = a
        args.append(nc.dram_tensor(f"in_{name}_dram", a.shape, _mybir.dt.from_np(a.dtype), kind="ExternalInput").ap())
    x = inputs['L0_attn_out']
    args.append(nc.dram_tensor("out_0_dram", x.shape, _mybir.dt.float32, kind="ExternalOutput").ap())
    preln_layer(nc, *args)
    r = _run(nc, [arrays], core_ids=[0])
    return r.results[0]["out_0_dram"]
```
